# Optimizing a Trainium2 kernel written in Bass

```python
import numpy as np
import jax
import jax.numpy as jnp

def _softmax(x, axis=-1):
    return jax.nn.softmax(x, axis=axis)

def _gelu(x):
    return jax.nn.gelu(x, approximate=True)

def _silu(x):
    return jax.nn.silu(x)

def _sigmoid(x):
    return jax.nn.sigmoid(x)

def _layernorm(x, axis=-1, eps=1e-05):
    m = jnp.mean(x, axis=axis, keepdims=True)
    v = jnp.var(x, axis=axis, keepdims=True)
    return (x - m) / jnp.sqrt(v + eps)

def _scatter_add(tgt, idx, src, axis=0):
    return tgt.at[idx].add(src)

def _segment_sum(src, seg, n):
    return jax.ops.segment_sum(src, seg, n)
kernel_name = 'mk_gnn_resnorm_d2_gnn_r8_e12472'

def setup_inputs(seed: int=0):
    np.random.seed(seed)
    _w = jnp.asarray

    def _rec_inputs():
        import jax
        import jax.numpy as jnp
        _gk = jax.random.key(seed)
        x = -0.0002117 + 1 * jax.random.normal(jax.random.fold_in(_gk, 1), (1250, 512), jnp.float32)
        _s = jax.random.randint(jax.random.fold_in(_gk, 2), (10000,), 0, 1250, jnp.int32)
        _d = jax.random.randint(jax.random.fold_in(_gk, 3), (10000,), 0, 1250, jnp.int32)
        _loop = jnp.arange(1250, dtype=jnp.int32)
        src = jnp.concatenate([_s, _d, _loop])
        dst = jnp.concatenate([_d, _s, _loop])
        _o = jnp.argsort(dst, stable=True)
        src = src[_o]
        dst = dst[_o]
        return (x, src, dst)
    x, src, dst = _rec_inputs()

    def _L0_gnn_setup():
        import jax, jax.numpy as jnp
        import numpy as np
        BN_EPS = 1e-05

        def batch_norm(h, gamma, beta):
            mu = jnp.mean(h, axis=0)
            var = jnp.var(h, axis=0)
            return (h - mu) * jax.lax.rsqrt(var + BN_EPS) * gamma + beta
        key = jax.random.key(seed)
        ks = jax.random.split(key, 6)
        N, E, dim = (6250, 200000, 512)
        hidden = dim * 2
        x = jax.random.normal(ks[0], (N, dim), dtype=jnp.float32)
        edge_index = jax.random.randint(ks[1], (2, E), 0, N, dtype=jnp.int64)
        s1 = 1.0 / np.sqrt(dim)
        s2 = 1.0 / np.sqrt(hidden)
        return {'x': x, 'edge_index': edge_index, 'eps': jnp.float32(0.0), 'W1': jax.random.uniform(ks[2], (dim, hidden), jnp.float32, -s1, s1), 'b1': jnp.zeros((hidden,), jnp.float32), 'g1': jnp.ones((hidden,), jnp.float32), 'be1': jnp.zeros((hidden,), jnp.float32), 'W2': jax.random.uniform(ks[3], (hidden, dim), jnp.float32, -s2, s2), 'b2': jnp.zeros((dim,), jnp.float32), 'g2': jnp.ones((dim,), jnp.float32), 'be2': jnp.zeros((dim,), jnp.float32)}
    _L0_gnn_all = _L0_gnn_setup()
    _L0_gnn_in = {k: v for k, v in _L0_gnn_all.items() if k in ('eps', 'W1', 'b1', 'g1', 'be1', 'W2', 'b2', 'g2', 'be2')}
    del _L0_gnn_all

    def _L1_gnn_setup():
        import jax, jax.numpy as jnp
        import numpy as np
        N = 6250
        E = 50000
        D_IN = 512
        D_HID = 256
        D_OUT = 512
        key = jax.random.key(seed)
        k1, k2, k3, k4 = jax.random.split(key, 4)
        x = jax.random.normal(k1, (N, D_IN), dtype=jnp.float32)
        edge_index = jax.random.randint(k2, (2, E), 0, N, dtype=jnp.int64)
        W1 = jax.random.normal(k3, (D_IN, D_HID), dtype=jnp.float32) * (1.0 / np.sqrt(D_IN))
        b1 = jnp.zeros((D_HID,), dtype=jnp.float32)
        W2 = jax.random.normal(k4, (D_HID, D_OUT), dtype=jnp.float32) * (1.0 / np.sqrt(D_HID))
        b2 = jnp.zeros((D_OUT,), dtype=jnp.float32)
        return {'x': x, 'edge_index': edge_index, 'W1': W1, 'b1': b1, 'W2': W2, 'b2': b2}
    _L1_gnn_all = _L1_gnn_setup()
    _L1_gnn_in = {k: v for k, v in _L1_gnn_all.items() if k in ('W1', 'b1', 'W2', 'b2')}
    del _L1_gnn_all
    return {'x': x, 'src': src, 'dst': dst, 'L0_gnn_eps': _L0_gnn_in['eps'], 'L0_gnn_W1': _L0_gnn_in['W1'], 'L0_gnn_b1': _L0_gnn_in['b1'], 'L0_gnn_g1': _L0_gnn_in['g1'], 'L0_gnn_be1': _L0_gnn_in['be1'], 'L0_gnn_W2': _L0_gnn_in['W2'], 'L0_gnn_b2': _L0_gnn_in['b2'], 'L0_gnn_g2': _L0_gnn_in['g2'], 'L0_gnn_be2': _L0_gnn_in['be2'], 'L1_gnn_W1': _L1_gnn_in['W1'], 'L1_gnn_b1': _L1_gnn_in['b1'], 'L1_gnn_W2': _L1_gnn_in['W2'], 'L1_gnn_b2': _L1_gnn_in['b2']}

def reference(x, src, dst, L0_gnn_eps, L0_gnn_W1, L0_gnn_b1, L0_gnn_g1, L0_gnn_be1, L0_gnn_W2, L0_gnn_b2, L0_gnn_g2, L0_gnn_be2, L1_gnn_W1, L1_gnn_b1, L1_gnn_W2, L1_gnn_b2):
    import jax
    import jax.numpy as jnp

    def _L0_gnn_ref(x, edge_index, eps, W1, b1, g1, be1, W2, b2, g2, be2):
        import jax, jax.numpy as jnp
        import numpy as np
        BN_EPS = 1e-05

        def batch_norm(h, gamma, beta):
            mu = jnp.mean(h, axis=0)
            var = jnp.var(h, axis=0)
            return (h - mu) * jax.lax.rsqrt(var + BN_EPS) * gamma + beta
        N = x.shape[0]
        src, dst = (edge_index[0], edge_index[1])
        agg = jax.ops.segment_sum(x[src], dst, num_segments=N)
        h = (1.0 + eps) * x + agg
        h = jax.nn.relu(batch_norm(h @ W1 + b1, g1, be1))
        h = h @ W2 + b2
        h = jax.nn.relu(batch_norm(h, g2, be2))
        return x + h

    def _L1_gnn_ref(x, edge_index, W1, b1, W2, b2):
        import jax, jax.numpy as jnp
        import numpy as np
        N = 6250
        E = 50000
        D_IN = 512
        D_HID = 256
        D_OUT = 512
        h = jax.nn.relu(x @ W1 + b1) @ W2 + b2
        row, col = (edge_index[0], edge_index[1])
        agg = jax.ops.segment_sum(h[col], row, num_segments=h.shape[0])
        return h + agg
    edge_index = jnp.stack([src, dst])
    x = _layernorm(x + _L0_gnn_ref(x, edge_index, L0_gnn_eps, L0_gnn_W1, L0_gnn_b1, L0_gnn_g1, L0_gnn_be1, L0_gnn_W2, L0_gnn_b2, L0_gnn_g2, L0_gnn_be2), axis=-1)
    x = _layernorm(x + _L1_gnn_ref(x, edge_index, L1_gnn_W1, L1_gnn_b1, L1_gnn_W2, L1_gnn_b2), axis=-1)
    return x

_drawn_inputs = setup_inputs


def setup_inputs(seed=0):
    import zlib

    import numpy as np

    out = dict(_drawn_inputs(seed))
    spreads = {'L0_gnn_b1': (0.0, 0.8),
     'L0_gnn_g1': (1.0, 0.2),
     'L0_gnn_be1': (0.0, 0.622),
     'L0_gnn_b2': (0.0, 0.8),
     'L0_gnn_g2': (1.0, 0.2),
     'L0_gnn_be2': (0.0, 0.1),
     'L1_gnn_b1': (0.0, 0.1),
     'L1_gnn_b2': (0.0, 0.1)}
    factors = {}
    for name, (base, spread) in spreads.items():
        noise = np.random.default_rng([zlib.crc32(name.encode()), seed]).standard_normal(out[name].shape)
        drawn = base * np.exp(spread * noise) if base else spread * noise
        out[name] = jnp.asarray(drawn.astype(out[name].dtype))
    for name, factor in factors.items():
        out[name] = (out[name] * factor).astype(out[name].dtype)
    return out
```

```python
from contextlib import ExitStack

import concourse.bass as bass
from concourse import mybir
from concourse.alu_op_type import AluOpType as ALU

F32 = mybir.dt.float32
F32R = mybir.dt.float32r
BF16 = mybir.dt.bfloat16
I32 = mybir.dt.int32
ACT = mybir.ActivationFunctionType
AX_X = mybir.AxisListType.X

P = 128
EPS = 1e-5
BANK = 512


def cdiv(a, b):
    return -(-a // b)


def gnn_kernel(nc, x, src, dst, eps, w1, b1, g1, be1, w2, b2, g2, be2, lw1, lb1, lw2, lb2, out, at_spill):
    N, D = x.shape
    (E,) = src.shape
    H = w1.shape[1]
    L = lw1.shape[1]
    NT = cdiv(N, P)
    rows = [min(P, N - P * k) for k in range(NT)]
    DT, HT, LT = D // P, H // P, L // P
    WIN = 10
    NW = N // WIN
    RUN = 2 * P
    WG = 5
    NG = NW // WG
    KEYS = NT * WIN
    GCOLS = WG * KEYS
    ER = NW
    EC = E // ER
    assert N % WIN == 0 and NW % WG == 0 and E % ER == 0 and GCOLS <= BANK and NW <= P
    CH = [(0, 250), (250, 750), (750, 1250)]
    CHG = [5, 15, 25]
    assert CH[-1][1] == N and all(g * WG * WIN == c[1] for g, c in zip(CHG, CH))
    BT = HT + DT
    BIG = 4096.0

    ctx = ExitStack()
    with ctx:
        def sem(name):
            return ctx.enter_context(nc.semaphore(name))

        base = cdiv(nc.sbuf_base, 64) * 64
        KB = 1024
        R_X, R_X2, R_AT = base, base + 20 * KB, base + 60 * KB
        R_H0 = R_AT + cdiv(NT * N * 4, 64) * 64
        R_W = R_H0 + 2 * DT * N * 4
        R_HOT = R_W + 32 * KB
        R_MISC = R_HOT + 2 * cdiv(N * 4, 64) * 64
        cursor = [R_MISC]

        def at(name, shape, dt, offset):
            return nc.alloc_sbuf_tensor_at(name, shape, dt, offset=offset)

        def misc(name, shape, dt):
            n = 4 if dt != BF16 else 2
            for s in shape[1:]:
                n *= s
            o = cursor[0]
            cursor[0] += cdiv(n, 32) * 32
            return at(name, shape, dt, o)

        xs = at("xs", [P, NT, D], F32, R_X)
        w1s = at("w1s", [P, DT, H], F32, R_X)
        w2s = at("w2s", [P, HT, D], F32, R_X)
        xh = at("xh", [P, NT, D], F32R, R_X2)
        xl = at("xl", [P, NT, D], F32R, R_X2 + 20 * KB)
        AT = at("AT", [P, NT, N], F32R, R_AT)
        h0h = at("h0h", [P, DT, N], F32R, R_H0)
        h0l = at("h0l", [P, DT, N], F32R, R_H0 + DT * N * 4)
        wh = at("wh", [P, HT, DT * P], F32R, R_W)
        wl = at("wl", [P, HT, DT * P], F32R, R_W + 16 * KB)
        hot_s = [at(f"hot_s{i}", [P, WG, P, 2], BF16, R_HOT + i * 4608) for i in range(2)]
        hot_k = [at(f"hot_k{i}", [P, WG, KEYS, 2], BF16, R_HOT + i * 4608 + 2560) for i in range(2)]
        a1h = [at(f"a1h{i}", [P, HT // 2, N], F32R, (R_X2, R_AT)[i]) for i in range(2)]
        a1l = [at(f"a1l{i}", [P, HT // 2, N], F32R, (R_X2, R_AT)[i] + 2 * N * HT) for i in range(2)]
        a32 = [at(f"a32_{i}", [P, N], F32, R_HOT + i * cdiv(N * 4, 64) * 64) for i in range(2)]
        h2 = at("h2", [P, DT, N], F32, R_H0)
        lws = at("lws", [P, DT, L], F32, R_H0 + DT * N * 4)
        lw2s = at("lw2s", [P, LT, D], F32, R_H0 + DT * N * 4 + 4 * KB)
        lw2h = at("lw2h", [P, LT, D], F32R, R_H0 + DT * N * 4 + 8 * KB)
        lw2l = at("lw2l", [P, LT, D], F32R, R_H0 + DT * N * 4 + 12 * KB)
        lw1h = at("lw1h", [P, DT, L], F32R, R_HOT)
        lw1l = at("lw1l", [P, DT, L], F32R, R_HOT + 4 * KB)
        ATr = [at("ATr0", [P, 8, N], F32, R_X2), at("ATr1", [P, NT - 8, N], F32, R_W + 20 * KB)]
        A = at("A", [P, NT, N], F32R, R_AT)
        uh = at("uh", [P, NT, L], F32R, R_W)
        ul = at("ul", [P, NT, L], F32R, R_W + 10 * KB)
        vh = at("vh", [P, LT, N], F32R, R_H0)
        vl = at("vl", [P, LT, N], F32R, R_H0 + cdiv(LT * N * 4, 64) * 64)
        nodes = at("nodes", [P, N], F32, R_H0)
        gen_src = at("gen_src", [P, EC], F32, R_H0 + 5 * KB)
        gen_s = at("gen_s", [P, P], BF16, R_H0 + 6 * KB)
        gen_d = at("gen_d", [P, N], BF16, R_H0 + 7 * KB)
        gen_0 = at("gen_0", [P, BANK], BF16, R_H0 + 10 * KB)
        TMP = [R_W]

        def tmp(name, shape, dt):
            o = TMP[0]
            TMP[0] += cdiv(shape[1] * 4, 32) * 32
            return at(name, shape, dt, o)

        dst_i = tmp("dst_i", [P, EC], I32)
        src_i = tmp("src_i", [P, EC], I32)
        dst_f = tmp("dst_f", [P, EC + 1], F32)
        prev_i = tmp("prev_i", [P, 1], I32)
        prev_f = tmp("prev_f", [P, 1], F32)
        win_row = tmp("win_row", [P, NW], F32)
        after = tmp("after", [P, NW], F32)
        below = tmp("below", [P, NW], F32)
        edge_row = tmp("edge_row", [P, NW], F32)
        less = tmp("less", [P, EC], F32)
        lo_n = tmp("lo_n", [P, 3], F32)
        start_i = tmp("start_i", [P, 1], I32)
        run_d = tmp("run_d", [P, RUN], I32)
        run_s = tmp("run_s", [P, RUN], I32)
        off = tmp("off", [P, RUN], F32)
        over = tmp("over", [P, RUN], F32)
        under = tmp("under", [P, RUN], F32)
        outside = tmp("outside", [P, RUN], F32)
        hi_i = tmp("hi_i", [P, RUN], I32)
        lo_i = tmp("lo_i", [P, RUN], I32)
        lo_f = tmp("lo_f", [P, RUN], F32)
        key0 = tmp("key0", [P, RUN], F32)
        key = tmp("key", [P, RUN], F32)
        n_out = tmp("n_out", [P, 1], F32)
        par_r = tmp("par_r", [P, P], F32)

        ident = misc("ident", [P, P], F32)
        iota2 = misc("iota2", [P, P, 2], BF16)
        keyT = misc("keyT", [P, NW, 2], BF16)
        loT = misc("loT", [P, NW, 2], BF16)
        win_col = misc("win_col", [P, 1], F32)
        ones = misc("ones", [P, 1], F32)
        one_r = misc("one_r", [1, P], F32R)
        flag = misc("flag", [1, 1], I32)
        eps_in = misc("eps_in", [P, 1], F32)
        eps1 = misc("eps1", [P, 1], F32)
        diag = misc("diag", [P, P], F32)
        diag_h = misc("diag_h", [P, P], F32R)
        diag_l = misc("diag_l", [P, P], F32R)
        epsc = misc("epsc", [P, 1], F32)
        par = misc("par", [P, 3 * BT], F32)
        lb1r = misc("lb1r", [1, L], F32)
        lb1h = misc("lb1h", [1, L], F32R)
        lb1l = misc("lb1l", [1, L], F32R)
        b2_all = misc("b2_all", [P, D], F32)
        deg = misc("deg", [P, NT], F32)
        deg1 = misc("deg1", [P, NT], F32)
        stats = misc("stats", [P, 18], F32)
        mv = misc("mv", [P, 2], F32)
        std = misc("std", [P, 1], F32)
        rstd = misc("rstd", [P, 1], F32)
        col = misc("col", [P, 4], F32)
        ln_s = misc("ln_s", [P, 2, 6], F32)
        ln_mv = misc("ln_mv", [P, 2, 2], F32)
        ln_std = misc("ln_std", [P, 2], F32)
        ln_r = misc("ln_r", [P, 2, 2], F32)
        u32 = misc("u32", [P, 2, L], F32)
        xth = at("xth", [P, 2, D], F32R, R_H0 + DT * N * 4)
        xtl = at("xtl", [P, 2, D], F32R, R_H0 + DT * N * 4 + 4 * KB)
        assert cursor[0] <= nc.sbuf_usable_end, (cursor[0], nc.sbuf_usable_end)

        ps = ctx.enter_context(nc.psum_tensor("ps", [P, 8, BANK], F32))

        dst_in, prev_in, src_in, eps_in_s, par_in, lb1_in, b2_in = (
            sem(n) for n in ("dst_in", "prev_in", "src_in", "eps_in_s", "par_in", "lb1_in", "b2_in"))
        x_in, w1_in, w2_in, lw_in, x_again = (sem(n) for n in ("x_in", "w1_in", "w2_in", "lw_in", "x_again"))
        spilled, AT_in, stored = sem("spilled"), sem("AT_in"), sem("stored")
        prev_set, const, ident_set = sem("prev_set"), sem("const"), sem("ident_set")
        dve = sem("dve")
        pool = sem("pool")
        rowsel, rowed, start_set, run_d_in, run_s_in = (
            sem(n) for n in ("rowsel", "rowed", "start_set", "run_d_in", "run_s_in"))
        keys_set, keys_T, counted, flag_set, par_T, par_set, diag_set = (
            sem(n) for n in ("keys_set", "keys_T", "counted", "flag_set", "par_T", "par_set", "diag_set"))
        xh_set, xl_set, w1h_set, w1l_set = (sem(n) for n in ("xh_set", "xl_set", "w1h_set", "w1l_set"))
        hot, built, AT_set = sem("hot"), sem("built"), sem("AT_set")
        gen_hot, gen_used, gen_sum, gen_copied = (
            sem(n) for n in ("gen_hot", "gen_used", "gen_sum", "gen_copied"))
        h0_sum, h0h_set, h0l_set = sem("h0_sum"), sem("h0h_set"), sem("h0l_set")
        z_sum, var_set, std_set, aff_set, act_set = (
            sem(n) for n in ("z_sum", "var_set", "std_set", "aff_set", "act_set"))
        a1h_set, a1l_set, a1l_last, w2h_set, w2l_set, deg_set = (
            sem(n) for n in ("a1h_set", "a1l_set", "a1l_last", "w2h_set", "w2l_set", "deg_set"))
        lwh_set, lwl_set = sem("lwh_set"), sem("lwl_set")
        h2_T, ln_var, ln_std_s, ln_aff, x1_set, x1_T, xth_set, xtl_set = (
            sem(n) for n in ("h2_T", "ln_var", "ln_std_s", "ln_aff", "x1_set", "x1_T", "xth_set", "xtl_set"))
        u_sum, u32_set, uh_set, ul_set, loops_set, A_T, A_set = (
            sem(n) for n in ("u_sum", "u32_set", "uh_set", "ul_set", "loops_set", "A_T", "A_set"))
        v_sum, vh_set, vl_set, base_set = sem("v_sum"), sem("vh_set"), sem("vl_set"), sem("base_set")
        y_sum, r2_set, ln2_var, ln2_std, ln2_aff, out_set = (
            sem(n) for n in ("y_sum", "r2_set", "ln2_var", "ln2_std", "ln2_aff", "out_set"))

        full = P * (N // P)

        def zbank(t, n):
            return 2 + 3 * (t % 2) + n

        def a1(part, kt):
            return part[kt // (HT // 2)][:, kt % (HT // 2), :]

        def atr(k):
            return ATr[0][:, k, :] if k < 8 else ATr[1][:, k - 8, :]

        NI = len(CH) * DT
        units = [(c * DT + d, k) for c in range(len(CH)) for d in range(DT) for k in range(NT)]
        per = DT * NT
        slot_units = [[] for _ in range(NG)]
        for c in range(len(CH) - 1):
            slots = list(range(CHG[c], CHG[c + 1]))
            for j in range(per):
                slot_units[slots[j * len(slots) // per]].append(units[c * per + j])
        tail_units = units[(len(CH) - 1) * per:]
        items_after = [[i for i, k in lot if k == NT - 1] for lot in slot_units]

        block = ctx.enter_context(nc.Block())

        @block.sync
        def _(sp):
            sp.dma_start(dst_i[0:ER, :], dst.rearrange("(p f) -> p f", p=ER)).then_inc(dst_in, 16)
            sp.wait_ge(prev_set, 1)
            with nc.allow_non_contiguous_dma("one column of the edge rows"):
                sp.dma_start(prev_i[1:ER, :], dst.rearrange("(p f) -> p f", p=ER)[0:ER - 1, EC - 1:EC]
                             ).then_inc(prev_in, 16)
            half = NT // 2
            sp.dma_start(xs[:, 0:half, :], x[0:half * P, :].rearrange("(t p) d -> p t d", p=P)).then_inc(x_in, 16)
            sp.dma_start(xs[:, half:NT - 1, :], x[half * P:full, :].rearrange("(t p) d -> p t d", p=P)
                         ).then_inc(x_in, 16)
            sp.dma_start(xs[0:rows[-1], NT - 1, :], x[full:N, :]).then_inc(x_in, 16)
            sp.dma_start(src_i[0:ER, :], src.rearrange("(p f) -> p f", p=ER)).then_inc(src_in, 16)
            sp.dma_start(b2_all[:, :], lb2.rearrange("(o d) -> o d", o=1).broadcast_to([P, D])).then_inc(b2_in, 16)
            sp.dma_start(lb1r[:, :], lb1.rearrange("(o d) -> o d", o=1)).then_inc(lb1_in, 16)
            sp.wait_ge(xh_set, NT)
            sp.wait_ge(xl_set, NT)
            sp.dma_start(w1s[:, :, :], w1.rearrange("(k p) n -> p k n", p=P)).then_inc(w1_in, 16)
            sp.wait_ge(w1h_set, 1)
            sp.wait_ge(w1l_set, DT)
            sp.dma_start(w2s[:, :, :], w2.rearrange("(k p) n -> p k n", p=P)).then_inc(w2_in, 16)
            sp.wait_ge(AT_set, NG)
            sp.dma_start(at_spill, AT[:, :, :].bitcast(F32).rearrange("p k n -> p (k n)")).then_inc(spilled, 16)
            sp.wait_ge(z_sum, HT)
            sp.dma_start(lws[:, :, :], lw1.rearrange("(k p) n -> p k n", p=P)).then_inc(lw_in, 16)
            sp.dma_start(lw2s[:, :, :], lw2.rearrange("(k p) n -> p k n", p=P)).then_inc(lw_in, 16)
            sp.wait_ge(w2h_set, HT)
            sp.wait_ge(w2l_set, HT)
            sp.dma_start(xs[:, 0:NT - 1, :], x[0:full, :].rearrange("(t p) d -> p t d", p=P)).then_inc(x_again, 16)
            sp.dma_start(xs[0:rows[-1], NT - 1, :], x[full:N, :]).then_inc(x_again, 16)
            sp.wait_ge(z_sum, BT)
            sp.wait_ge(spilled, 16)
            sp.dma_start(ATr[0][:, :, :], at_spill[:, 0:8 * N].rearrange("p (k n) -> p k n", n=N)).then_inc(AT_in, 16)
            sp.dma_start(ATr[1][:, :, :], at_spill[:, 8 * N:NT * N].rearrange("p (k n) -> p k n", n=N)
                         ).then_inc(AT_in, 16)
            for k in range(NT):
                sp.wait_ge(out_set, k + 1)
                sp.dma_start(out[P * k:P * k + rows[k], :], xs[0:rows[k], k, :]).then_inc(stored, 16)
            sp.wait_ge(stored, 16 * NT)
            sp.wait_ge(src_in, 16)

        @block.gpsimd
        def _(pl):
            n = [0]

            def link(ins):
                n[0] += 1
                ins.then_inc(pool, 1)
                pl.wait_ge(pool, n[0])

            nc.gpsimd.memset(prev_i[:, :], -1).then_inc(prev_set, 1)
            nc.gpsimd.iota(win_row[:, :], pattern=[[WIN, NW]], base=0, channel_multiplier=0,
                           allow_small_or_imprecise_dtypes=True).then_inc(const, 1)
            nc.gpsimd.iota(win_col[:, :], pattern=[[0, 1]], base=0, channel_multiplier=WIN,
                           allow_small_or_imprecise_dtypes=True).then_inc(const, 1)
            nc.gpsimd.memset(dst_f[:, EC:EC + 1], float(EC)).then_inc(const, 1)
            nc.gpsimd.memset(ones[:, :], 1.0).then_inc(const, 1)
            nc.gpsimd.iota(iota2[:, :, :], pattern=[[1, P], [0, 2]], base=0, channel_multiplier=0,
                           allow_small_or_imprecise_dtypes=True).then_inc(const, 1)
            link(nc.gpsimd.memset(ident[:, :], 0.0))
            nc.gpsimd.affine_select(out=ident[:, :], in_=ident[:, :], compare_op=ALU.not_equal, fill=1.0,
                                    base=0, pattern=[[-1, P]], channel_multiplier=1).then_inc(ident_set, 1)
            nc.gpsimd.memset(epsc[:, :], EPS).then_inc(const, 1)
            nc.gpsimd.memset(one_r[:, :].bitcast(F32), 1.0).then_inc(const, 1)
            nc.gpsimd.iota(nodes[:, :], pattern=[[1, N]], base=0, channel_multiplier=0,
                           allow_small_or_imprecise_dtypes=True).then_inc(const, 1)
            nc.gpsimd.memset(gen_0[:, :], 0.0).then_inc(const, 1)
            pl.wait_ge(start_set, 1)
            nc.gpsimd.indirect_dma_start(run_d[0:NW, :], None, dst.rearrange("(e o) -> e o", o=1),
                                         bass.IndirectOffsetOnAxis(ap=start_i[0:NW, :], axis=0)).then_inc(run_d_in, 16)
            nc.gpsimd.indirect_dma_start(run_s[0:NW, :], None, src.rearrange("(e o) -> e o", o=1),
                                         bass.IndirectOffsetOnAxis(ap=start_i[0:NW, :], axis=0)).then_inc(run_s_in, 16)
            for k in range(NT):
                pl.wait_ge(xh_set, k + 1)
                nc.gpsimd.tensor_tensor(xl[0:rows[k], k, :], xs[0:rows[k], k, :],
                                        xh[0:rows[k], k, :].bitcast(F32), ALU.subtract).then_inc(xl_set, 1)
            pl.wait_ge(w1h_set, 1)
            for d in range(DT):
                nc.gpsimd.tensor_tensor(wl[:, :, d * P:d * P + P], w1s[:, d, :].rearrange("p (m c) -> p m c", c=P),
                                        wh[:, :, d * P:d * P + P].bitcast(F32), ALU.subtract).then_inc(w1l_set, 1)
            for t in range(HT):
                pl.wait_ge(w2h_set, t + 1)
                nc.gpsimd.tensor_tensor(wl[:, t, :], w2s[:, t, :], wh[:, t, :].bitcast(F32),
                                        ALU.subtract).then_inc(w2l_set, 1)
                if t < HT - 1:
                    pl.wait_ge(a1h_set, t + 1)
                    nc.gpsimd.tensor_tensor(a1(a1l, t), a32[t % 2][:, :], a1(a1h, t).bitcast(F32),
                                            ALU.subtract).then_inc(a1l_set, 1)
            pl.wait_ge(lwh_set, 3)
            nc.gpsimd.tensor_tensor(lw1l[:, :, :], lws[:, :, :], lw1h[:, :, :].bitcast(F32),
                                    ALU.subtract).then_inc(lwl_set, 1)
            nc.gpsimd.tensor_tensor(lw2l[:, :, :], lw2s[:, :, :], lw2h[:, :, :].bitcast(F32),
                                    ALU.subtract).then_inc(lwl_set, 1)
            nc.gpsimd.tensor_tensor(lb1l[:, :], lb1r[:, :], lb1h[:, :].bitcast(F32),
                                    ALU.subtract).then_inc(lwl_set, 1)

            def loops(k):
                s = atr(k)[0:rows[k], P * k:P * k + rows[k]]
                nc.gpsimd.tensor_tensor(s, s, ident[0:rows[k], 0:rows[k]], ALU.add).then_inc(loops_set, 1)

            def u_low(k):
                pl.wait_ge(uh_set, k + 1)
                nc.gpsimd.tensor_tensor(ul[0:rows[k], k, :], u32[0:rows[k], k % 2, :],
                                        uh[0:rows[k], k, :].bitcast(F32), ALU.subtract).then_inc(ul_set, 1)

            for k in range(NT):
                u_low(k)
                if k == 3:
                    pl.wait_ge(AT_in, 32)
                    for j in range(NT):
                        loops(j)

        @block.scalar
        def _(act):
            for r, (v, t) in enumerate(((b1, HT), (g1, HT), (be1, HT), (b2, DT), (g2, DT), (be2, DT))):
                r0 = r * HT if r < 3 else 3 * HT + (r - 3) * DT
                act.dma_start(par_r[r0:r0 + t, :], v.rearrange("(t p) -> t p", p=P)).then_inc(par_in, 16)
            act.dma_start(eps_in[:, :], eps.rearrange("(o d) -> o d", o=1).broadcast_to([P, 1])).then_inc(eps_in_s, 16)
            for k in range(NT):
                if k == 0 or k == NT // 2 or k == NT - 1:
                    act.wait_ge(x_in, 48)
                nc.scalar.activation(xh[0:rows[k], k, :], xs[0:rows[k], k, :], ACT.Copy).then_inc(xh_set, 1)

            def group_out(g):
                act.wait_ge(built, g + 1)
                nc.scalar.activation(
                    AT[:, :, g * WG * WIN:(g + 1) * WG * WIN].rearrange("p k (w d) -> p k w d", w=WG),
                    ps[:, g % 2, 0:GCOLS].rearrange("p (w k d) -> p k w d", w=WG, k=NT), ACT.Copy
                ).then_inc(AT_set, 1)

            def h0_high(i):
                c, d = divmod(i, DT)
                c0, c1 = CH[c]
                act.wait_ge(h0_sum, i + 1)
                nc.scalar.activation(h0h[:, d, c0:c1], ps[:, 2 + i % 6, 0:c1 - c0], ACT.Copy).then_inc(h0h_set, 1)

            act.wait_ge(flag_set, 1)
            bad = act.value_load(flag[0:1, 0:1], min_val=0, max_val=1)
            with act.If(bad == 0):
                for g in range(NG):
                    group_out(g)
                    if g == 8:
                        act.wait_ge(w1_in, 16)
                        nc.scalar.activation(wh[:, :, :].rearrange("p m (k c) -> p k m c", c=P),
                                             w1s[:, :, :].rearrange("p k (m c) -> p k m c", c=P),
                                             ACT.Copy).then_inc(w1h_set, 1)
                    for i in items_after[g]:
                        h0_high(i)
            with act.Else():
                act.wait_ge(AT_set, NG)
                act.wait_ge(w1_in, 16)
                nc.scalar.activation(wh[:, :, :].rearrange("p m (k c) -> p k m c", c=P),
                                     w1s[:, :, :].rearrange("p k (m c) -> p k m c", c=P),
                                     ACT.Copy).then_inc(w1h_set, 1)
                for i in range(NI - DT):
                    h0_high(i)
            for i in range(NI - DT, NI):
                h0_high(i)

            def affine(t):
                act.wait_ge(var_set, t + 1)
                nc.scalar.activation(std[:, :], mv[:, 1:2], ACT.Sqrt, bias=epsc[:, :]).then_inc(std_set, 1)
                act.wait_ge(aff_set, t + 1)
                o = a32[t % 2][:, :] if t < HT else h2[:, t - HT, :]
                if t < HT and t >= 2:
                    act.wait_ge(a1l_set, t - 1)
                if t == HT:
                    act.wait_ge(z_sum, HT)
                z0 = zbank(t, 0)
                n0 = CH[0][1]
                nc.scalar.activation(o[:, 0:n0], ps[:, z0, 0:n0], ACT.Relu, bias=col[:, 3:4],
                                     scale=col[:, 2:3]).then_inc(act_set, 1)
                nc.scalar.activation(o[:, n0:N].rearrange("p (b c) -> p b c", b=2),
                                     ps[:, z0 + 1:z0 + 3, 0:(N - n0) // 2], ACT.Relu, bias=col[:, 3:4],
                                     scale=col[:, 2:3]).then_inc(act_set, 1)

            def w2_high(t):
                act.wait_ge(z_sum, t + 1)
                if t == 0:
                    act.wait_ge(w2_in, 16)
                nc.scalar.activation(wh[:, t, :], w2s[:, t, :], ACT.Copy).then_inc(w2h_set, 1)

            for t in range(HT):
                affine(t)
                if t == 0:
                    act.wait_ge(h0_sum, NI)
                if t == HT // 2:
                    act.wait_ge(spilled, 16)
                    act.wait_ge(deg_set, 1)
                act.wait_ge(act_set, 2 * t + 2)
                nc.scalar.activation(a1(a1h, t), a32[t % 2][:, :], ACT.Copy).then_inc(a1h_set, 1)
                w2_high(t)
            act.wait_ge(lw_in, 32)
            act.wait_ge(lb1_in, 16)
            act.wait_ge(a1l_set, HT - 1)
            act.wait_ge(a1l_last, 1)
            nc.scalar.activation(lw1h[:, :, :], lws[:, :, :], ACT.Copy).then_inc(lwh_set, 1)
            nc.scalar.activation(lw2h[:, :, :], lw2s[:, :, :], ACT.Copy).then_inc(lwh_set, 1)
            nc.scalar.activation(lb1h[:, :], lb1r[:, :], ACT.Copy).then_inc(lwh_set, 1)
            for t in range(HT, BT):
                affine(t)

            def ln_root(k):
                act.wait_ge(ln_var, k + 1)
                r = rows[k]
                nc.scalar.activation(ln_std[0:r, k % 2:k % 2 + 1], ln_mv[0:r, k % 2, 1:2], ACT.Sqrt,
                                     bias=epsc[0:r, :]).then_inc(ln_std_s, 1)

            def ln_apply(k):
                act.wait_ge(ln_aff, k + 1)
                r = rows[k]
                nc.scalar.activation(xs[0:r, k, :], xs[0:r, k, :], ACT.Identity, bias=ln_r[0:r, k % 2, 1:2],
                                     scale=ln_r[0:r, k % 2, 0:1]).then_inc(x1_set, 1)

            def xt_high(k):
                r = rows[k]
                act.wait_ge(x1_T, k + 1)
                if k == 0:
                    act.wait_ge(lwl_set, 3)
                if k >= 2:
                    act.wait_ge(u_sum, k - 1)
                nc.scalar.activation(xth[:, k % 2, :].rearrange("p (d c) -> p d c", c=P)[:, :, 0:r],
                                     ps[:, 2 + k % 2, :].rearrange("p (d c) -> p d c", c=P)[:, :, 0:r],
                                     ACT.Copy).then_inc(xth_set, 1)

            def u_relu(k):
                r = rows[k]
                act.wait_ge(u_sum, k + 1)
                if k >= 2:
                    act.wait_ge(ul_set, k - 1)
                nc.scalar.activation(u32[0:r, k % 2, :], ps[0:r, 4 + k % 2, 0:L], ACT.Relu).then_inc(u32_set, 1)
                act.wait_ge(u32_set, k + 1)
                nc.scalar.activation(uh[0:r, k, :], u32[0:r, k % 2, :], ACT.Copy).then_inc(uh_set, 1)

            def A_out(j):
                kd, q = divmod(j, 3)
                act.wait_ge(A_T, j + 1)
                c0, c1 = q * BANK, min(N, (q + 1) * BANK)
                nc.scalar.activation(A[0:rows[kd], kd, c0:c1], ps[0:rows[kd], 6 + j % 2, 0:c1 - c0],
                                     ACT.Copy).then_inc(A_set, 1)

            for s in range(NT + 3):
                if 0 <= s - 1 < NT:
                    ln_apply(s - 1)
                if s < NT:
                    ln_root(s)
                if 0 <= s - 2 < NT:
                    xt_high(s - 2)
                if 0 <= s - 3 < NT:
                    u_relu(s - 3)
                if s >= 7:
                    for j in range(5 * (s - 7), 5 * (s - 6)):
                        A_out(j)
            for i in range(LT * len(CH)):
                m, c = divmod(i, len(CH))
                c0, c1 = CH[c]
                act.wait_ge(v_sum, i + 1)
                nc.scalar.activation(vh[:, m, c0:c1], ps[:, i, 0:c1 - c0], ACT.Copy).then_inc(vh_set, 1)

            def ln2_root(k):
                act.wait_ge(ln2_var, k + 1)
                r = rows[k]
                nc.scalar.activation(ln_std[0:r, k % 2:k % 2 + 1], ln_mv[0:r, k % 2, 1:2], ACT.Sqrt,
                                     bias=epsc[0:r, :]).then_inc(ln2_std, 1)

            def ln2_apply(k):
                act.wait_ge(ln2_aff, k + 1)
                r = rows[k]
                nc.scalar.activation(xs[0:r, k, :], xs[0:r, k, :], ACT.Identity, bias=ln_r[0:r, k % 2, 1:2],
                                     scale=ln_r[0:r, k % 2, 0:1]).then_inc(out_set, 1)

            for s in range(NT + 1):
                if s >= 1:
                    ln2_apply(s - 1)
                if s < NT:
                    ln2_root(s)

        @block.vector
        def _(v):
            n = [0]

            def link(ins):
                n[0] += 1
                ins.then_inc(dve, 1)
                v.wait_ge(dve, n[0])

            v.wait_ge(dst_in, 16)
            v.wait_ge(const, 3)
            link(nc.vector.tensor_copy(dst_f[0:ER, 0:EC], dst_i[0:ER, :]))
            v.wait_ge(prev_in, 16)
            link(nc.vector.tensor_copy(prev_f[0:ER, :], prev_i[0:ER, :]))
            link(nc.vector.tensor_scalar(after[0:ER, :], win_row[0:ER, :], prev_f[0:ER, 0:1], None, ALU.is_gt))
            link(nc.vector.tensor_scalar(below[0:ER, :], win_row[0:ER, :], dst_f[0:ER, EC - 1:EC], None, ALU.is_gt))
            nc.vector.tensor_tensor(edge_row[0:ER, :], after[0:ER, :], below[0:ER, :],
                                    ALU.subtract).then_inc(rowsel, 1)
            v.wait_ge(rowed, 1)
            link(nc.vector.tensor_scalar(less[0:NW, :], ps[0:NW, 2, 0:EC], win_col[0:NW, 0:1], 0.0, ALU.is_lt,
                                         ALU.add, accum_out=lo_n[0:NW, 0:1]))
            link(nc.vector.tensor_tensor(lo_n[0:NW, 1:2], lo_n[0:NW, 0:1], ps[0:NW, 2, EC:EC + 1], ALU.add))
            link(nc.vector.tensor_scalar(lo_n[0:NW, 2:3], lo_n[0:NW, 1:2], float(E - RUN), 0.0, ALU.min, ALU.max))
            nc.vector.tensor_copy(start_i[0:NW, :], lo_n[0:NW, 2:3]).then_inc(start_set, 1)
            v.wait_ge(eps_in_s, 16)
            v.wait_ge(ident_set, 1)
            link(nc.vector.tensor_scalar(eps1[:, :], eps_in[:, :], 1.0, None, ALU.add))
            link(nc.vector.tensor_scalar(diag[:, :], ident[:, :], eps1[:, 0:1], None, ALU.mult))
            link(nc.vector.tensor_copy(diag_h[:, :], diag[:, :]))
            nc.vector.tensor_tensor(diag_l[:, :], diag[:, :], diag_h[:, :].bitcast(F32),
                                    ALU.subtract).then_inc(diag_set, 1)
            v.wait_ge(par_T, 1)
            nc.vector.tensor_copy(par[:, :], ps[:, 4, 0:3 * BT]).then_inc(par_set, 1)
            v.wait_ge(run_d_in, 16)
            link(nc.vector.tensor_scalar(off[0:NW, :], run_d[0:NW, :], win_col[0:NW, 0:1], None, ALU.subtract))
            nc.vector.tensor_scalar(over[0:NW, :], off[0:NW, :], float(WIN), BIG, ALU.is_ge, ALU.mult).then_inc(dve, 1)
            n[0] += 1
            link(nc.vector.tensor_scalar(under[0:NW, :], off[0:NW, :], 0.0, BIG, ALU.is_lt, ALU.mult))
            link(nc.vector.tensor_tensor_reduce(out=outside[0:NW, :], in0=over[0:NW, :], in1=under[0:NW, :], scale=1.0,
                                                scalar=0.0, op0=ALU.add, op1=ALU.add, accum_out=n_out[0:NW, :]))
            v.wait_ge(run_s_in, 16)
            link(nc.vector.tensor_scalar(hi_i[0:NW, :], run_s[0:NW, :], 7, None, ALU.logical_shift_right))
            link(nc.vector.scalar_tensor_tensor(out=key0[0:NW, :], in0=hi_i[0:NW, :], scalar=float(WIN),
                                                in1=off[0:NW, :], op0=ALU.mult, op1=ALU.add))
            nc.vector.tensor_tensor(key[0:NW, :], key0[0:NW, :], outside[0:NW, :], ALU.add).then_inc(keys_set, 1)
            link(nc.vector.tensor_scalar(lo_i[0:NW, :], run_s[0:NW, :], P - 1, None, ALU.bitwise_and))
            nc.vector.tensor_copy(lo_f[0:NW, :], lo_i[0:NW, :]).then_inc(keys_set, 1)
            v.wait_ge(keys_T, 1)
            q = ps[:, 3, 0:4 * NW].rearrange("p (a c w) -> p a w c", a=2, c=2)
            link(nc.vector.tensor_copy(keyT[:, :, :], q[:, 0]))
            link(nc.vector.tensor_copy(loT[:, :, :], q[:, 1]))
            v.wait_ge(counted, 1)
            nc.vector.tensor_scalar(flag[0:1, :], ps[0:1, 5, 0:1], BIG * (NW * RUN - E), None,
                                    ALU.not_equal).then_inc(flag_set, 1)

            def one_hots(g):
                if g >= 2:
                    v.wait_ge(built, g - 1)
                w = slice(g * WG, (g + 1) * WG)
                nc.vector.tensor_tensor(
                    hot_s[g % 2][:, :, :, :], iota2[:, None, :, :].broadcast_to([P, WG, P, 2]),
                    loT[:, w, None, :].broadcast_to([P, WG, P, 2]), ALU.is_equal).then_inc(hot, 1)
                nc.vector.tensor_tensor(
                    hot_k[g % 2][:, :, :, :], iota2[:, None, 0:KEYS, :].broadcast_to([P, WG, KEYS, 2]),
                    keyT[:, w, None, :].broadcast_to([P, WG, KEYS, 2]), ALU.is_equal).then_inc(hot, 1)

            def h0_low(i):
                c, d = divmod(i, DT)
                c0, c1 = CH[c]
                v.wait_ge(h0h_set, i + 1)
                nc.vector.tensor_tensor(h0l[:, d, c0:c1], ps[:, 2 + i % 6, 0:c1 - c0],
                                        h0h[:, d, c0:c1].bitcast(F32), ALU.subtract).then_inc(h0l_set, 1)

            v.wait_ge(flag_set, 1)
            bad = v.value_load(flag[0:1, 0:1], min_val=0, max_val=1)
            with v.If(bad == 0):
                late = []
                for g in range(NG):
                    one_hots(g)
                    while late and late[0][0] <= g:
                        h0_low(late.pop(0)[1])
                    late += [(g + 2, i) for i in items_after[g]]
                for _, i in late:
                    h0_low(i)
            with v.Else():
                v.wait_ge(src_in, 16)
                v.wait_ge(const, 9)
                nc.vector.tensor_copy(gen_src[0:ER, :], src_i[0:ER, :]).then_inc(gen_copied, 1)
                with v.Fori(0, NT) as h:
                    with v.Fori(0, EC) as f:
                        v.wait_ge(gen_copied, h * 4 + 1)
                        v.wait_ge(gen_used, h * (EC + 1) + f + 1)
                        nc.vector.tensor_scalar(gen_s[0:ER, :], iota2[0:ER, :, 0], gen_src[0:ER, bass.ds(f, 1)],
                                                None, ALU.is_equal).then_inc(gen_hot, 1)
                        nc.vector.tensor_scalar(gen_d[0:ER, :], nodes[0:ER, :], dst_f[0:ER, bass.ds(f, 1)],
                                                None, ALU.is_equal).then_inc(gen_hot, 1)
                    v.wait_ge(gen_sum, h + 1)
                    for c, (c0, c1) in enumerate(CH):
                        nc.vector.tensor_copy(AT[:, bass.ds(h, 1), c0:c1],
                                              ps[:, 2 + c, None, 0:c1 - c0]).then_inc(gen_copied, 1)
                    nc.vector.tensor_scalar(gen_src[0:ER, :], gen_src[0:ER, :], -float(P), None,
                                            ALU.add).then_inc(gen_copied, 1)
                v.wait_ge(gen_copied, 4 * NT + 1)
                nc.vector.memset(n_out[:, :], 0.0).then_inc(AT_set, NG)
                for i in range(NI - DT):
                    h0_low(i)
            for i in range(NI - DT, NI):
                h0_low(i)

            def batch_norm(t):
                v.wait_ge(z_sum, t + 1)
                if t == 0:
                    v.wait_ge(par_set, 1)
                i = t if t < HT else t + 2 * HT
                step = HT if t < HT else DT
                b, g, be = (par[:, i + j * step:i + j * step + 1] for j in range(3))
                for c, (c0, c1) in enumerate(CH):
                    link(nc.vector.bn_stats(stats[:, 6 * c:6 * c + 6], ps[:, zbank(t, c), 0:c1 - c0]))
                nc.vector.bn_aggr(mv[:, :], stats[:, :]).then_inc(var_set, 1)
                v.wait_ge(var_set, t + 1)
                link(nc.vector.tensor_tensor(col[:, 0:1], mv[:, 0:1], b, ALU.add))
                link(nc.vector.tensor_tensor(col[:, 1:2], b, col[:, 0:1], ALU.subtract))
                v.wait_ge(std_set, t + 1)
                link(nc.vector.reciprocal(rstd[:, :], std[:, :]))
                if t >= 1:
                    v.wait_ge(act_set, 2 * t)
                link(nc.vector.tensor_tensor(col[:, 2:3], rstd[:, :], g, ALU.mult))
                nc.vector.scalar_tensor_tensor(out=col[:, 3:4], in0=col[:, 1:2], scalar=col[:, 2:3], in1=be,
                                               op0=ALU.mult, op1=ALU.add).then_inc(aff_set, 1)

            degs = [0, 3, 6, 8, 10]
            for t in range(HT):
                batch_norm(t)
                if t < len(degs) - 1:
                    a, b = degs[t], degs[t + 1]
                    link(nc.vector.tensor_reduce(deg[:, a:b], AT[:, a:b, :].bitcast(F32), AX_X, ALU.add))
                    if t == len(degs) - 2:
                        nc.vector.tensor_scalar(deg1[:, :], deg[:, :], 1.0, None, ALU.add).then_inc(deg_set, 1)
            v.wait_ge(a1h_set, HT)
            nc.vector.tensor_tensor(a1(a1l, HT - 1), a32[(HT - 1) % 2][:, :], a1(a1h, HT - 1).bitcast(F32),
                                    ALU.subtract).then_inc(a1l_last, 1)
            for t in range(HT, BT):
                batch_norm(t)

            def ln_stats(k):
                r = rows[k]
                v.wait_ge(h2_T, k + 1)
                link(nc.vector.scalar_tensor_tensor(out=xs[0:r, k, :], in0=xs[0:r, k, :], scalar=2.0,
                                                    in1=ps[0:r, k % 2, :], op0=ALU.mult, op1=ALU.add))
                link(nc.vector.bn_stats(ln_s[0:r, k % 2, :], xs[0:r, k, :]))
                nc.vector.bn_aggr(ln_mv[0:r, k % 2, :], ln_s[0:r, k % 2, :]).then_inc(ln_var, 1)

            def ln_scale(k, root, done):
                r = rows[k]
                v.wait_ge(root, k + 1)
                link(nc.vector.reciprocal(ln_r[0:r, k % 2, 0:1], ln_std[0:r, k % 2:k % 2 + 1]))
                nc.vector.scalar_tensor_tensor(out=ln_r[0:r, k % 2, 1:2], in0=ln_mv[0:r, k % 2, 0:1], scalar=-1.0,
                                               in1=ln_r[0:r, k % 2, 0:1], op0=ALU.mult, op1=ALU.mult).then_inc(done, 1)

            def xt_low(k):
                r = rows[k]
                v.wait_ge(xth_set, k + 1)
                nc.vector.tensor_tensor(xtl[:, k % 2, :].rearrange("p (d c) -> p d c", c=P)[:, :, 0:r],
                                        ps[:, 2 + k % 2, :].rearrange("p (d c) -> p d c", c=P)[:, :, 0:r],
                                        xth[:, k % 2, :].rearrange("p (d c) -> p d c", c=P)[:, :, 0:r].bitcast(F32),
                                        ALU.subtract).then_inc(xtl_set, 1)

            v.wait_ge(x_again, 32)
            for s in range(NT + 2):
                if 0 <= s - 1 < NT:
                    ln_scale(s - 1, ln_std_s, ln_aff)
                if s < NT:
                    if s >= 2:
                        v.wait_ge(x1_set, s - 1)
                    ln_stats(s)
                if 0 <= s - 2 < NT:
                    xt_low(s - 2)
            def base(k):
                r = rows[k]
                v.wait_ge(x1_T, k + 1)
                nc.vector.scalar_tensor_tensor(out=xs[0:r, k, :], in0=b2_all[0:r, :], scalar=deg1[0:r, k:k + 1],
                                               in1=xs[0:r, k, :], op0=ALU.mult, op1=ALU.add).then_inc(base_set, 1)

            v.wait_ge(b2_in, 16)
            v.wait_ge(deg_set, 1)
            for i in range(LT * len(CH)):
                for k in range(2 * i, min(NT, 2 * i + 2)):
                    base(k)
                m, c = divmod(i, len(CH))
                c0, c1 = CH[c]
                v.wait_ge(vh_set, i + 1)
                nc.vector.tensor_tensor(vl[:, m, c0:c1], ps[:, i, 0:c1 - c0], vh[:, m, c0:c1].bitcast(F32),
                                        ALU.subtract).then_inc(vl_set, 1)

            def ln2_stats(k):
                r = rows[k]
                v.wait_ge(y_sum, k + 1)
                v.wait_ge(base_set, k + 1)
                nc.vector.tensor_tensor(xs[0:r, k, :], ps[0:r, (6 + k) % 8, :], xs[0:r, k, :], ALU.add).then_inc(r2_set, 1)
                v.wait_ge(r2_set, k + 1)
                link(nc.vector.bn_stats(ln_s[0:r, k % 2, :], xs[0:r, k, :]))
                nc.vector.bn_aggr(ln_mv[0:r, k % 2, :], ln_s[0:r, k % 2, :]).then_inc(ln2_var, 1)

            for s in range(NT + 1):
                if s >= 1:
                    ln_scale(s - 1, ln2_std, ln2_aff)
                if s < NT:
                    if s >= 2:
                        v.wait_ge(out_set, s - 1)
                    ln2_stats(s)

        @block.tensor
        def _(pe):
            mm = nc.tensor.matmul
            pe.wait_ge(rowsel, 1)
            mm(ps[0:NW, 2, 0:EC], edge_row[0:ER, :], dst_f[0:ER, 0:EC], start=True, stop=True)
            mm(ps[0:NW, 2, EC:EC + 1], below[0:ER, :], dst_f[0:ER, EC:EC + 1], start=True, stop=True).then_inc(rowed, 1)
            pe.wait_ge(ident_set, 1)
            pe.wait_ge(par_in, 6 * 16)
            nc.tensor.transpose(ps[:, 4, 0:3 * BT], par_r[0:3 * BT, :], ident[0:3 * BT, 0:3 * BT]).then_inc(par_T, 1)
            pe.wait_ge(keys_set, 2)
            for a, s in enumerate((key, lo_f)):
                for c in range(2):
                    o = (2 * a + c) * NW
                    last = nc.tensor.transpose(ps[:, 3, o:o + NW], s[0:NW, c * P:c * P + P], ident[0:NW, 0:NW])
            last.then_inc(keys_T, 1)
            pe.wait_ge(const, 9)
            mm(ps[0:1, 5, 0:1], n_out[0:NW, :], ones[0:NW, :], start=True, stop=True).then_inc(counted, 1)

            def build(g):
                pe.wait_ge(hot, 2 * g + 2)
                if g >= 2:
                    pe.wait_ge(AT_set, g - 1)
                for w in range(WG):
                    for c in range(2):
                        last = mm(ps[:, g % 2, w * KEYS:(w + 1) * KEYS], hot_s[g % 2][:, w, :, c],
                                  hot_k[g % 2][:, w, :, c], start=(c == 0), stop=(c == 1))
                last.then_inc(built, 1)

            def aggregate(i, k):
                c, d = divmod(i, DT)
                c0, c1 = CH[c]
                r = rows[k]
                o = ps[:, 2 + i % 6, 0:c1 - c0]
                if k == 0:
                    pe.wait_ge(AT_set, CHG[c])
                    if i == 0:
                        pe.wait_ge(diag_set, 1)
                    if i >= 6:
                        pe.wait_ge(h0l_set, i - 5)
                if i == 0:
                    pe.wait_ge(xl_set, k + 1)
                ds = slice(d * P, d * P + P)
                a, b = max(c0, P * k), min(c1, P * k + r)
                parts = [(xh, AT[0:r, k, c0:c1], o), (xl, AT[0:r, k, c0:c1], o)]
                if a < b:
                    dc = slice(a - P * k, b - P * k)
                    oo = ps[:, 2 + i % 6, a - c0:b - c0]
                    parts += [(xh, diag_h[0:r, dc], oo), (xl, diag_h[0:r, dc], oo), (xh, diag_l[0:r, dc], oo)]
                for j, (part, rhs, oo) in enumerate(parts):
                    last = mm(oo, part[0:r, k, ds], rhs, start=(k == 0 and j == 0),
                              stop=(k == NT - 1 and j == len(parts) - 1), skip_group_check=True)
                if k == NT - 1:
                    last.then_inc(h0_sum, 1)

            pe.wait_ge(flag_set, 1)
            bad = pe.value_load(flag[0:1, 0:1], min_val=0, max_val=1)
            with pe.If(bad == 0):
                for g in range(NG):
                    build(g)
                    for u in slot_units[g]:
                        aggregate(*u)
            with pe.Else():
                with pe.Fori(0, NT) as h:
                    pe.wait_ge(gen_copied, h * 4 + 1)
                    for c, (c0, c1) in enumerate(CH):
                        last = mm(ps[:, 2 + c, 0:c1 - c0], gen_0[0:ER, 0:P], gen_0[0:ER, 0:c1 - c0], start=True,
                                  stop=False, skip_group_check=True)
                    last.then_inc(gen_used, 1)
                    with pe.Fori(0, EC) as f:
                        pe.wait_ge(gen_hot, (h * EC + f) * 2 + 2)
                        for c, (c0, c1) in enumerate(CH):
                            last = mm(ps[:, 2 + c, 0:c1 - c0], gen_s[0:ER, :], gen_d[0:ER, c0:c1], start=False,
                                      stop=False, skip_group_check=True)
                        last.then_inc(gen_used, 1)
                    for c, (c0, c1) in enumerate(CH):
                        last = mm(ps[:, 2 + c, 0:c1 - c0], gen_0[0:ER, 0:P], gen_0[0:ER, 0:c1 - c0], start=False,
                                  stop=True, skip_group_check=True)
                    last.then_inc(gen_sum, 1)
                for u in units[0:(len(CH) - 1) * per]:
                    aggregate(*u)
            for u in tail_units:
                aggregate(*u)

            pe.wait_ge(w1l_set, DT)
            for t in range(HT):
                if t >= 2:
                    pe.wait_ge(act_set, 2 * t - 2)
                for c, (c0, c1) in enumerate(CH):
                    if t == 0:
                        pe.wait_ge(h0l_set, max(DT * (c + 1), 7 + c))
                    for d in range(DT):
                        for j, (w, h) in enumerate(((wh, h0h), (wl, h0h), (wh, h0l))):
                            last = mm(ps[:, zbank(t, c), 0:c1 - c0], w[:, t, d * P:d * P + P], h[:, d, c0:c1],
                                      start=(d == 0 and j == 0), stop=(d == DT - 1 and j == 2))
                last.then_inc(z_sum, 1)

            for t in range(HT, BT):
                m = t - HT
                pe.wait_ge(act_set, 2 * t - 2)
                for k in range(HT):
                    if t == HT:
                        pe.wait_ge(w2l_set, k + 1)
                        if k < HT - 1:
                            pe.wait_ge(a1l_set, k + 1)
                        else:
                            pe.wait_ge(a1l_last, 1)
                    for j, (w, a) in enumerate(((wh, a1h), (wl, a1h), (wh, a1l))):
                        for c, (c0, c1) in enumerate(CH):
                            last = mm(ps[:, zbank(t, c), 0:c1 - c0], w[:, k, m * P:m * P + P],
                                      a1(a, k)[:, c0:c1], start=(k == 0 and j == 0),
                                      stop=(k == HT - 1 and j == 2))
                last.then_inc(z_sum, 1)

            def h2_rows(k):
                r = rows[k]
                if k == 0:
                    pe.wait_ge(act_set, 2 * BT)
                if k >= 2:
                    pe.wait_ge(ln_var, k - 1)
                for m in range(DT):
                    last = nc.tensor.transpose(ps[0:r, k % 2, m * P:m * P + P], h2[:, m, P * k:P * k + r], ident[:, :])
                last.then_inc(h2_T, 1)

            def x1_cols(k):
                r = rows[k]
                pe.wait_ge(x1_set, k + 1)
                if k >= 2:
                    pe.wait_ge(xtl_set, k - 1)
                for d in range(DT):
                    last = nc.tensor.transpose(ps[:, 2 + k % 2, d * P:d * P + r], xs[0:r, k, d * P:d * P + P],
                                               ident[0:r, 0:r])
                last.then_inc(x1_T, 1)

            def hidden(k):
                r = rows[k]
                pe.wait_ge(xtl_set, k + 1)
                if k == 0:
                    pe.wait_ge(lwl_set, 3)
                if k >= 2:
                    pe.wait_ge(u32_set, k - 1)
                o = ps[0:r, 4 + k % 2, 0:L]
                mm(o, one_r[:, 0:r], lb1h[:, :], start=True, stop=False)
                mm(o, one_r[:, 0:r], lb1l[:, :], start=False, stop=False)
                for d in range(DT):
                    for j, (xt, w) in enumerate(((xth, lw1h), (xtl, lw1h), (xth, lw1l))):
                        last = mm(o, xt[:, k % 2, d * P:d * P + r], w[:, d, :], start=False,
                                  stop=(d == DT - 1 and j == 2))
                last.then_inc(u_sum, 1)

            def A_rows(j):
                kd, q = divmod(j, 3)
                if j == 0:
                    pe.wait_ge(loops_set, NT)
                if j >= 2:
                    pe.wait_ge(A_set, j - 1)
                for hi in range(4 * q, min(NT, 4 * q + 4)):
                    o = (hi - 4 * q) * P
                    last = nc.tensor.transpose(ps[0:rows[kd], 6 + j % 2, o:o + rows[hi]],
                                               atr(hi)[0:rows[hi], P * kd:P * kd + rows[kd]],
                                               ident[0:rows[hi], 0:rows[hi]])
                last.then_inc(A_T, 1)

            for s in range(NT + 3):
                if s < NT:
                    h2_rows(s)
                if 0 <= s - 2 < NT:
                    x1_cols(s - 2)
                if 0 <= s - 3 < NT:
                    hidden(s - 3)
                if s >= 7:
                    for j in range(5 * (s - 7), 5 * (s - 6)):
                        A_rows(j)

            for m in range(LT):
                for c, (c0, c1) in enumerate(CH):
                    i = m * len(CH) + c
                    for k in range(NT):
                        r = rows[k]
                        if i == 0:
                            pe.wait_ge(ul_set, k + 1)
                            pe.wait_ge(A_set, 3 * k + 3)
                        for j, part in enumerate((uh, ul)):
                            last = mm(ps[:, i, 0:c1 - c0], part[0:r, k, m * P:m * P + P], A[0:r, k, c0:c1],
                                      start=(k == 0 and j == 0), stop=(k == NT - 1 and j == 1))
                    last.then_inc(v_sum, 1)

            for k in range(NT):
                r = rows[k]
                ch = next(c for c, (c0, c1) in enumerate(CH) if P * k + r <= c1)
                pe.wait_ge(vl_set, (LT - 1) * len(CH) + ch + 1)
                b = (6 + k) % 8
                if k >= 2:
                    pe.wait_ge(vl_set, LT * len(CH))
                if k >= 8:
                    pe.wait_ge(r2_set, k - 7)
                for m in range(LT):
                    for j, (part, w) in enumerate(((vh, lw2h), (vl, lw2h), (vh, lw2l))):
                        last = mm(ps[0:r, b, :], part[:, m, P * k:P * k + r], w[:, m, :],
                                  start=(m == 0 and j == 0), stop=(m == LT - 1 and j == 2))
                last.then_inc(y_sum, 1)


_INS = ["x", "src", "dst", "L0_gnn_eps", "L0_gnn_W1", "L0_gnn_b1", "L0_gnn_g1", "L0_gnn_be1", "L0_gnn_W2",
        "L0_gnn_b2", "L0_gnn_g2", "L0_gnn_be2", "L1_gnn_W1", "L1_gnn_b1", "L1_gnn_W2", "L1_gnn_b2"]


def kernel(**inputs):
    import numpy as np
    import concourse.bacc as bacc
    from concourse.bass_utils import run_bass_kernel_spmd

    nc = bacc.Bacc("TRN2", target_bir_lowering=False, num_devices=1)
    arrays, args = {}, []
    for name in _INS:
        a = np.ascontiguousarray(inputs[name]).reshape(np.shape(inputs[name]) or (1,))
        arrays[f"in_{name}"] = a
        args.append(nc.dram_tensor(f"in_{name}", a.shape, mybir.dt.from_np(a.dtype), kind="ExternalInput").ap())
    n, d = inputs["x"].shape
    args.append(nc.dram_tensor("out_0", (n, d), F32, kind="ExternalOutput").ap())
    args.append(nc.dram_tensor("at_spill", (P, cdiv(n, P) * n), F32, kind="Internal").ap())
    gnn_kernel(nc, *args)
    r = run_bass_kernel_spmd(nc, [arrays], core_ids=[0])
    return r.results[0]["out_0"]
```

```python
from contextlib import ExitStack

import concourse.bass as bass
from concourse import mybir
from concourse.alu_op_type import AluOpType as ALU

F32 = mybir.dt.float32
F32R = mybir.dt.float32r
BF16 = mybir.dt.bfloat16
I32 = mybir.dt.int32
ACT = mybir.ActivationFunctionType
AX_X = mybir.AxisListType.X

P = 128
EPS = 1e-5
BANK = 512


def cdiv(a, b):
    return -(-a // b)


def gnn_kernel(nc, x, src, dst, eps, w1, b1, g1, be1, w2, b2, g2, be2, lw1, lb1, lw2, lb2, out, a_spill):
    N, D = x.shape
    (E,) = src.shape
    H = w1.shape[1]
    L = lw1.shape[1]
    NT = cdiv(N, P)
    rows = [min(P, N - P * k) for k in range(NT)]
    DT, HT, LT = D // P, H // P, L // P
    WIN = 10
    NW = N // WIN
    RUN = 2 * P
    WG = 5
    NG = NW // WG
    KEYS = NT * WIN
    GCOLS = WG * KEYS
    ER = NW
    EC = E // ER
    assert N % WIN == 0 and NW % WG == 0 and E % ER == 0 and GCOLS <= BANK and NW <= P
    CH = [(0, 250), (250, 750), (750, 1250)]
    CHG = [5, 15, 25]
    assert CH[-1][1] == N and all(g * WG * WIN == c[1] for g, c in zip(CHG, CH))
    BT = HT + DT
    BIG = 4096.0

    ctx = ExitStack()
    with ctx:
        def sem(name):
            return ctx.enter_context(nc.semaphore(name))

        base = cdiv(nc.sbuf_base, 64) * 64
        KB = 1024
        R_X, R_X2, R_AT = base, base + 20 * KB, base + 60 * KB
        R_H0 = R_AT + cdiv(NT * N * 4, 64) * 64
        R_W = R_H0 + 2 * DT * N * 4
        R_HOT = R_W + 32 * KB
        R_MISC = R_HOT + 2 * cdiv(N * 4, 64) * 64
        cursor = [R_MISC]

        def at(name, shape, dt, offset):
            return nc.alloc_sbuf_tensor_at(name, shape, dt, offset=offset)

        def misc(name, shape, dt):
            n = 4 if dt != BF16 else 2
            for s in shape[1:]:
                n *= s
            o = cursor[0]
            cursor[0] += cdiv(n, 32) * 32
            return at(name, shape, dt, o)

        xs = at("xs", [P, NT, D], F32, R_X)
        w1s = at("w1s", [P, DT, H], F32, R_X)
        w2s = at("w2s", [P, HT, D], F32, R_X)
        xh = at("xh", [P, NT, D], F32R, R_X2)
        xl = at("xl", [P, NT, D], F32R, R_X2 + 20 * KB)
        AT = at("AT", [P, NT, N], F32R, R_AT)
        h0h = at("h0h", [P, DT, N], F32R, R_H0)
        h0l = at("h0l", [P, DT, N], F32R, R_H0 + DT * N * 4)
        wh = at("wh", [P, HT, DT * P], F32R, R_W)
        wl = at("wl", [P, HT, DT * P], F32R, R_W + 16 * KB)
        hot_s = [at(f"hot_s{i}", [P, WG, P, 2], BF16, R_HOT + i * 4608) for i in range(2)]
        hot_k = [at(f"hot_k{i}", [P, WG, KEYS, 2], BF16, R_HOT + i * 4608 + 2560) for i in range(2)]
        a1h = [at(f"a1h{i}", [P, HT // 2, N], F32R, (R_X2, R_AT)[i]) for i in range(2)]
        a1l = [at(f"a1l{i}", [P, HT // 2, N], F32R, (R_X2, R_AT)[i] + 2 * N * HT) for i in range(2)]
        a32 = [at(f"a32_{i}", [P, N], F32, R_HOT + i * cdiv(N * 4, 64) * 64) for i in range(2)]
        h2 = at("h2", [P, DT, N], F32, R_H0)
        lws = at("lws", [P, DT, L], F32, R_H0 + DT * N * 4)
        lw2s = at("lw2s", [P, LT, D], F32, R_H0 + DT * N * 4 + 4 * KB)
        lw2h = at("lw2h", [P, LT, D], F32R, R_H0 + DT * N * 4 + 8 * KB)
        lw2l = at("lw2l", [P, LT, D], F32R, R_H0 + DT * N * 4 + 12 * KB)
        lw1h = at("lw1h", [P, DT, L], F32R, R_HOT)
        lw1l = at("lw1l", [P, DT, L], F32R, R_HOT + 4 * KB)
        A = [at("A0", [P, 8, N], F32R, R_X2), at("A1", [P, NT - 8, N], F32R, R_AT)]
        uh = at("uh", [P, NT, L], F32R, R_W)
        ul = at("ul", [P, NT, L], F32R, R_W + 10 * KB)
        vh = at("vh", [P, LT * N], F32R, R_H0)
        vl = at("vl", [P, LT * N], F32R, R_H0 + cdiv(LT * N * 4, 64) * 64)
        nodes = at("nodes", [P, N], F32, R_H0)
        gen_src = at("gen_src", [P, EC], F32, R_H0 + 5 * KB)
        gen_s = at("gen_s", [P, P], BF16, R_H0 + 6 * KB)
        gen_d = at("gen_d", [P, N], BF16, R_H0 + 7 * KB)
        gen_0 = at("gen_0", [P, BANK], BF16, R_H0 + 10 * KB)
        TMP = [R_W]

        def tmp(name, shape, dt):
            o = TMP[0]
            TMP[0] += cdiv(shape[1] * 4, 32) * 32
            return at(name, shape, dt, o)

        dst_i = tmp("dst_i", [P, EC], I32)
        src_i = tmp("src_i", [P, EC], I32)
        dst_f = tmp("dst_f", [P, EC + 1], F32)
        prev_i = tmp("prev_i", [P, 1], I32)
        prev_f = tmp("prev_f", [P, 1], F32)
        win_row = tmp("win_row", [P, NW], F32)
        after = tmp("after", [P, NW], F32)
        below = tmp("below", [P, NW], F32)
        edge_row = tmp("edge_row", [P, NW], F32)
        less = tmp("less", [P, EC], F32)
        lo_n = tmp("lo_n", [P, 3], F32)
        start_i = tmp("start_i", [P, 1], I32)
        run_d = tmp("run_d", [P, RUN], I32)
        run_s = tmp("run_s", [P, RUN], I32)
        off = tmp("off", [P, RUN], F32)
        over = tmp("over", [P, RUN], F32)
        under = tmp("under", [P, RUN], F32)
        outside = tmp("outside", [P, RUN], F32)
        hi_i = tmp("hi_i", [P, RUN], I32)
        lo_i = tmp("lo_i", [P, RUN], I32)
        lo_f = tmp("lo_f", [P, RUN], F32)
        key0 = tmp("key0", [P, RUN], F32)
        key = tmp("key", [P, RUN], F32)
        n_out = tmp("n_out", [P, 1], F32)
        par_r = tmp("par_r", [P, P], F32)

        ident = misc("ident", [P, P], F32)
        iota2 = misc("iota2", [P, P, 2], BF16)
        keyT = misc("keyT", [P, NW, 2], BF16)
        loT = misc("loT", [P, NW, 2], BF16)
        win_col = misc("win_col", [P, 1], F32)
        ones = misc("ones", [P, 1], F32)
        one_r = misc("one_r", [1, P], F32R)
        flag = misc("flag", [1, 1], I32)
        eps_in = misc("eps_in", [P, 1], F32)
        eps1 = misc("eps1", [P, 1], F32)
        diag = misc("diag", [P, P], F32)
        diag_h = misc("diag_h", [P, P], F32R)
        diag_l = misc("diag_l", [P, P], F32R)
        epsc = misc("epsc", [P, 1], F32)
        par = misc("par", [P, 3 * BT], F32)
        lb1r = misc("lb1r", [1, L], F32)
        lb1h = misc("lb1h", [1, L], F32R)
        lb1l = misc("lb1l", [1, L], F32R)
        b2_all = misc("b2_all", [P, D], F32)
        deg1 = misc("deg1", [P, NT], F32)
        stats = misc("stats", [P, 18], F32)
        mv = misc("mv", [P, 2], F32)
        std = misc("std", [P, 1], F32)
        rstd = misc("rstd", [P, 1], F32)
        col = misc("col", [P, 4], F32)
        ln_s = misc("ln_s", [P, NT, 6], F32)
        ln_mv = misc("ln_mv", [P, NT, 2], F32)
        ln_m = misc("ln_m", [P, NT, 2], F32)
        ln_q = misc("ln_q", [P, NT], F32)
        ln_std = misc("ln_std", [P, NT], F32)
        ln_r = misc("ln_r", [P, NT, 2], F32)
        u32 = misc("u32", [P, 2, L], F32)
        xth = at("xth", [P, 2, D], F32R, R_H0 + DT * N * 4)
        xtl = at("xtl", [P, 2, D], F32R, R_H0 + DT * N * 4 + 4 * KB)
        stage = [at(f"stage{i}", [P, BANK], F32, R_X + (16 + 2 * i) * KB) for i in range(2)]
        stage += [u32[:, :, :].rearrange("p a b -> p (a b)")]
        stage += [misc(f"stage{i}", [P, BANK], F32) for i in range(3, 5)]
        assert cursor[0] <= nc.sbuf_usable_end, (cursor[0], nc.sbuf_usable_end)

        ps = ctx.enter_context(nc.psum_tensor("ps", [P, 8, BANK], F32))

        dst_in, prev_in, src_in, eps_in_s, par_in, lb1_in, b2_in = (
            sem(n) for n in ("dst_in", "prev_in", "src_in", "eps_in_s", "par_in", "lb1_in", "b2_in"))
        x_in, w1_in, w2_in, lw_in, x_again = (sem(n) for n in ("x_in", "w1_in", "w2_in", "lw_in", "x_again"))
        stored = sem("stored")
        spilled = [sem(f"spilled{i}") for i in range(len(stage))]
        A_in = [sem(f"A_in{i}") for i in range(cdiv(NT, 2))]
        prev_set, const, ident_set = sem("prev_set"), sem("const"), sem("ident_set")
        dve = sem("dve")
        pool = sem("pool")
        rowsel, rowed, start_set, run_d_in, run_s_in = (
            sem(n) for n in ("rowsel", "rowed", "start_set", "run_d_in", "run_s_in"))
        keys_set, keys_T, counted, flag_set, par_T, par_set, diag_set = (
            sem(n) for n in ("keys_set", "keys_T", "counted", "flag_set", "par_T", "par_set", "diag_set"))
        xh_set, xl_set, w1h_set, w1l_set = (sem(n) for n in ("xh_set", "xl_set", "w1h_set", "w1l_set"))
        hot, built, AT_set = sem("hot"), sem("built"), sem("AT_set")
        gen_hot, gen_used, gen_sum, gen_copied = (
            sem(n) for n in ("gen_hot", "gen_used", "gen_sum", "gen_copied"))
        h0_sum, h0h_set, h0l_set = sem("h0_sum"), sem("h0h_set"), sem("h0l_set")
        z_sum, z_part, var_set, std_set, aff_set, act_set = (
            sem(n) for n in ("z_sum", "z_part", "var_set", "std_set", "aff_set", "act_set"))
        a1h_set, a1l_set, a1l_last, w2h_set, w2l_set, deg_set = (
            sem(n) for n in ("a1h_set", "a1l_set", "a1l_last", "w2h_set", "w2l_set", "deg_set"))
        lwh_set, lwl_set = sem("lwh_set"), sem("lwl_set")
        h2_T, ln_var, ln_std_s, ln_aff, x1_set, x1_T, xth_set, xtl_set = (
            sem(n) for n in ("h2_T", "ln_var", "ln_std_s", "ln_aff", "x1_set", "x1_T", "xth_set", "xtl_set"))
        u_sum, u32_set, uh_set, ul_set = (sem(n) for n in ("u_sum", "u32_set", "uh_set", "ul_set"))
        loops_set, A_T, A_act, A_dve, a1_first_used = (
            sem(n) for n in ("loops_set", "A_T", "A_act", "A_dve", "a1_first_used"))
        v_sum, vh_set, vl_set, base_set = sem("v_sum"), sem("vh_set"), sem("vl_set"), sem("base_set")
        y_sum, ln2_mean, ln2_var, ln2_std, ln2_aff, out_even, out_odd = (
            sem(n) for n in ("y_sum", "ln2_mean", "ln2_var", "ln2_std", "ln2_aff", "out_even", "out_odd"))

        full = P * (N // P)

        def zbank(t, n):
            return 2 + 3 * (t % 2) + n

        def a1(part, kt):
            return part[kt // (HT // 2)][:, kt % (HT // 2), :]

        def a_rows(k):
            return A[0][:, k, :] if k < 8 else A[1][:, k - 8, :]

        AQ = cdiv(N, BANK)
        NJ = NT * AQ
        JT = 6
        assert NJ % JT == 0 and NJ // JT <= HT // 2 + 1 and NJ % len(stage) == 0

        VB = cdiv(LT * N, BANK)
        V0 = 8 - VB
        v_width = [min(BANK, LT * N - BANK * b) for b in range(VB)]
        v_blocks = [(m, b, max(0, b * BANK - m * N), min(N, (b + 1) * BANK - m * N))
                    for m in range(LT) for b in range(m * N // BANK, ((m + 1) * N - 1) // BANK + 1)]
        v_first = {b: m for m, b, _, _ in reversed(v_blocks)}
        v_order = []
        for k in range(NT):
            for m in range(LT):
                for f in (m * N + P * k, m * N + P * k + rows[k] - 1):
                    if f // BANK not in v_order:
                        v_order.append(f // BANK)

        def v_needed(k):
            return 1 + max(v_order.index(f // BANK) for m in range(LT)
                           for f in (m * N + P * k, m * N + P * k + rows[k] - 1))

        def part_cols(j):
            q = j % AQ
            return q * BANK, min(N, (q + 1) * BANK)

        def part_out(j):
            c0, c1 = part_cols(j)
            r = rows[j // AQ]
            return stage[j % len(stage)][0:r, 0:c1 - c0], ps[0:r, j % 2, 0:c1 - c0]

        NI = len(CH) * DT
        units = [(c * DT + d, k) for c in range(len(CH)) for d in range(DT) for k in range(NT)]
        per = DT * NT
        slot_units = [[] for _ in range(NG)]
        for c in range(len(CH) - 1):
            slots = list(range(CHG[c], CHG[c + 1]))
            for j in range(per):
                slot_units[slots[j * len(slots) // per]].append(units[c * per + j])
        tail_units = units[(len(CH) - 1) * per:]
        items_after = [[i for i, k in lot if k == NT - 1] for lot in slot_units]

        block = ctx.enter_context(nc.Block())

        @block.sync
        def _(sp):
            sp.dma_start(dst_i[0:ER, :], dst.rearrange("(p f) -> p f", p=ER)).then_inc(dst_in, 16)
            sp.wait_ge(prev_set, 1)
            with nc.allow_non_contiguous_dma("one column of the edge rows"):
                sp.dma_start(prev_i[1:ER, :], dst.rearrange("(p f) -> p f", p=ER)[0:ER - 1, EC - 1:EC]
                             ).then_inc(prev_in, 16)
            half = NT // 2
            sp.dma_start(xs[:, 0:half, :], x[0:half * P, :].rearrange("(t p) d -> p t d", p=P)).then_inc(x_in, 16)
            sp.dma_start(xs[:, half:NT - 1, :], x[half * P:full, :].rearrange("(t p) d -> p t d", p=P)
                         ).then_inc(x_in, 16)
            sp.dma_start(xs[0:rows[-1], NT - 1, :], x[full:N, :]).then_inc(x_in, 16)
            sp.dma_start(src_i[0:ER, :], src.rearrange("(p f) -> p f", p=ER)).then_inc(src_in, 16)
            sp.dma_start(b2_all[:, :], lb2.rearrange("(o d) -> o d", o=1).broadcast_to([P, D])).then_inc(b2_in, 16)
            sp.dma_start(lb1r[:, :], lb1.rearrange("(o d) -> o d", o=1)).then_inc(lb1_in, 16)
            sp.wait_ge(xh_set, NT)
            sp.wait_ge(xl_set, NT)
            sp.dma_start(w1s[:, :, :], w1.rearrange("(k p) n -> p k n", p=P)).then_inc(w1_in, 16)
            sp.wait_ge(w1h_set, 1)
            sp.wait_ge(w1l_set, DT)
            sp.dma_start(w2s[:, :, :], w2.rearrange("(k p) n -> p k n", p=P)).then_inc(w2_in, 16)
            for j in range(NJ):
                sp.wait_ge((A_act, A_dve)[j % 2], j // 2 + 1)
                kd = j // AQ
                c0, c1 = part_cols(j)
                sp.dma_start(a_spill[P * kd:P * kd + rows[kd], c0:c1], part_out(j)[0]
                             ).then_inc(spilled[j % len(stage)], 16)
            sp.wait_ge(z_sum, HT)
            sp.dma_start(lws[:, :, :], lw1.rearrange("(k p) n -> p k n", p=P)).then_inc(lw_in, 16)
            sp.dma_start(lw2s[:, :, :], lw2.rearrange("(k p) n -> p k n", p=P)).then_inc(lw_in, 16)
            for i in range(len(stage)):
                sp.wait_ge(spilled[i], 16 * (NJ // len(stage)))
            sp.wait_ge(w2h_set, HT)
            sp.wait_ge(w2l_set, HT)
            sp.dma_start(xs[:, 0:NT - 1, :], x[0:full, :].rearrange("(t p) d -> p t d", p=P)).then_inc(x_again, 16)
            sp.dma_start(xs[0:rows[-1], NT - 1, :], x[full:N, :]).then_inc(x_again, 16)
            sp.wait_ge(a1_first_used, 1)
            for i, k in enumerate(range(0, NT, 2)):
                if k == 8:
                    sp.wait_ge(z_part, len(CH))
                if rows[k + 1] == P:
                    sp.dma_start(A[0][:, k:k + 2, :].bitcast(F32), a_spill[P * k:P * k + 2 * P, :].rearrange(
                        "(t p) n -> p t n", p=P)).then_inc(A_in[i], 16)
                else:
                    sp.dma_start(a_rows(k).bitcast(F32), a_spill[P * k:P * k + P, :]).then_inc(A_in[i], 16)
                    sp.dma_start(a_rows(k + 1)[0:rows[k + 1], :].bitcast(F32), a_spill[P * k + P:N, :]).then_inc(A_in[i], 16)
            for k in range(NT):
                sp.wait_ge((out_even, out_odd)[k % 2], k // 2 + 1)
                sp.dma_start(out[P * k:P * k + rows[k], :], xs[0:rows[k], k, :]).then_inc(stored, 16)
            sp.wait_ge(stored, 16 * NT)
            sp.wait_ge(src_in, 16)

        @block.gpsimd
        def _(pl):
            n = [0]

            def link(ins):
                n[0] += 1
                ins.then_inc(pool, 1)
                pl.wait_ge(pool, n[0])

            nc.gpsimd.memset(prev_i[:, :], -1).then_inc(prev_set, 1)
            nc.gpsimd.iota(win_row[:, :], pattern=[[WIN, NW]], base=0, channel_multiplier=0,
                           allow_small_or_imprecise_dtypes=True).then_inc(const, 1)
            nc.gpsimd.iota(win_col[:, :], pattern=[[0, 1]], base=0, channel_multiplier=WIN,
                           allow_small_or_imprecise_dtypes=True).then_inc(const, 1)
            nc.gpsimd.memset(dst_f[:, EC:EC + 1], float(EC)).then_inc(const, 1)
            nc.gpsimd.memset(ones[:, :], 1.0).then_inc(const, 1)
            nc.gpsimd.iota(iota2[:, :, :], pattern=[[1, P], [0, 2]], base=0, channel_multiplier=0,
                           allow_small_or_imprecise_dtypes=True).then_inc(const, 1)
            link(nc.gpsimd.memset(ident[:, :], 0.0))
            nc.gpsimd.affine_select(out=ident[:, :], in_=ident[:, :], compare_op=ALU.not_equal, fill=1.0,
                                    base=0, pattern=[[-1, P]], channel_multiplier=1).then_inc(ident_set, 1)
            nc.gpsimd.memset(epsc[:, :], EPS).then_inc(const, 1)
            nc.gpsimd.memset(one_r[:, :].bitcast(F32), 1.0).then_inc(const, 1)
            nc.gpsimd.iota(nodes[:, :], pattern=[[1, N]], base=0, channel_multiplier=0,
                           allow_small_or_imprecise_dtypes=True).then_inc(const, 1)
            nc.gpsimd.memset(gen_0[:, :], 0.0).then_inc(const, 1)
            pl.wait_ge(start_set, 1)
            nc.gpsimd.indirect_dma_start(run_d[0:NW, :], None, dst.rearrange("(e o) -> e o", o=1),
                                         bass.IndirectOffsetOnAxis(ap=start_i[0:NW, :], axis=0)).then_inc(run_d_in, 16)
            nc.gpsimd.indirect_dma_start(run_s[0:NW, :], None, src.rearrange("(e o) -> e o", o=1),
                                         bass.IndirectOffsetOnAxis(ap=start_i[0:NW, :], axis=0)).then_inc(run_s_in, 16)
            for k in range(NT):
                pl.wait_ge(xh_set, k + 1)
                nc.gpsimd.tensor_tensor(xl[0:rows[k], k, :], xs[0:rows[k], k, :],
                                        xh[0:rows[k], k, :].bitcast(F32), ALU.subtract).then_inc(xl_set, 1)
            pl.wait_ge(w1h_set, 1)
            for d in range(DT):
                nc.gpsimd.tensor_tensor(wl[:, :, d * P:d * P + P], w1s[:, d, :].rearrange("p (m c) -> p m c", c=P),
                                        wh[:, :, d * P:d * P + P].bitcast(F32), ALU.subtract).then_inc(w1l_set, 1)
            pl.wait_ge(h0_sum, NI)
            for k in range(NT):
                own = AT[0:rows[k], k, P * k:P * k + rows[k]]
                nc.gpsimd.tensor_tensor(own, own.bitcast(F32), ident[0:rows[k], 0:rows[k]], ALU.add
                                        ).then_inc(loops_set, 1)
            for t in range(HT):
                pl.wait_ge(w2h_set, t + 1)
                nc.gpsimd.tensor_tensor(wl[:, t, :], w2s[:, t, :], wh[:, t, :].bitcast(F32),
                                        ALU.subtract).then_inc(w2l_set, 1)
                if t < HT - 1:
                    pl.wait_ge(a1h_set, t + 1)
                    nc.gpsimd.tensor_tensor(a1(a1l, t), a32[t % 2][:, :], a1(a1h, t).bitcast(F32),
                                            ALU.subtract).then_inc(a1l_set, 1)
            pl.wait_ge(lwh_set, 3)
            nc.gpsimd.tensor_tensor(lw1l[:, :, :], lws[:, :, :], lw1h[:, :, :].bitcast(F32),
                                    ALU.subtract).then_inc(lwl_set, 1)
            nc.gpsimd.tensor_tensor(lw2l[:, :, :], lw2s[:, :, :], lw2h[:, :, :].bitcast(F32),
                                    ALU.subtract).then_inc(lwl_set, 1)
            nc.gpsimd.tensor_tensor(lb1l[:, :], lb1r[:, :], lb1h[:, :].bitcast(F32),
                                    ALU.subtract).then_inc(lwl_set, 1)

            def u_low(k):
                pl.wait_ge(uh_set, k + 1)
                nc.gpsimd.tensor_tensor(ul[0:rows[k], k, :], u32[0:rows[k], k % 2, :],
                                        uh[0:rows[k], k, :].bitcast(F32), ALU.subtract).then_inc(ul_set, 1)

            for k in range(NT):
                u_low(k)
            for k in range(0, NT, 2):
                pl.wait_ge(ln2_aff, k + 1)
                r = rows[k]
                nc.gpsimd.tensor_scalar(xs[0:r, k, :], xs[0:r, k, :], ln_r[0:r, k, 0:1], ln_r[0:r, k, 1:2],
                                        ALU.mult, ALU.add).then_inc(out_even, 1)

        @block.scalar
        def _(act):
            for r, (v, t) in enumerate(((b1, HT), (g1, HT), (be1, HT), (b2, DT), (g2, DT), (be2, DT))):
                r0 = r * HT if r < 3 else 3 * HT + (r - 3) * DT
                act.dma_start(par_r[r0:r0 + t, :], v.rearrange("(t p) -> t p", p=P)).then_inc(par_in, 16)
            act.dma_start(eps_in[:, :], eps.rearrange("(o d) -> o d", o=1).broadcast_to([P, 1])).then_inc(eps_in_s, 16)
            for k in range(NT):
                if k == 0 or k == NT // 2 or k == NT - 1:
                    act.wait_ge(x_in, 48)
                nc.scalar.activation(xh[0:rows[k], k, :], xs[0:rows[k], k, :], ACT.Copy).then_inc(xh_set, 1)

            def group_out(g):
                act.wait_ge(built, g + 1)
                nc.scalar.activation(
                    AT[:, :, g * WG * WIN:(g + 1) * WG * WIN].rearrange("p k (w d) -> p k w d", w=WG),
                    ps[:, g % 2, 0:GCOLS].rearrange("p (w k d) -> p k w d", w=WG, k=NT), ACT.Copy
                ).then_inc(AT_set, 1)

            def h0_high(i):
                c, d = divmod(i, DT)
                c0, c1 = CH[c]
                act.wait_ge(h0_sum, i + 1)
                nc.scalar.activation(h0h[:, d, c0:c1], ps[:, 2 + i % 6, 0:c1 - c0], ACT.Copy).then_inc(h0h_set, 1)

            act.wait_ge(flag_set, 1)
            bad = act.value_load(flag[0:1, 0:1], min_val=0, max_val=1)
            with act.If(bad == 0):
                for g in range(NG):
                    group_out(g)
                    if g == 8:
                        act.wait_ge(w1_in, 16)
                        nc.scalar.activation(wh[:, :, :].rearrange("p m (k c) -> p k m c", c=P),
                                             w1s[:, :, :].rearrange("p k (m c) -> p k m c", c=P),
                                             ACT.Copy).then_inc(w1h_set, 1)
                    for i in items_after[g]:
                        h0_high(i)
            with act.Else():
                act.wait_ge(AT_set, NG)
                act.wait_ge(w1_in, 16)
                nc.scalar.activation(wh[:, :, :].rearrange("p m (k c) -> p k m c", c=P),
                                     w1s[:, :, :].rearrange("p k (m c) -> p k m c", c=P),
                                     ACT.Copy).then_inc(w1h_set, 1)
                for i in range(NI - DT):
                    h0_high(i)
            for i in range(NI - DT, NI):
                h0_high(i)

            def affine(t):
                act.wait_ge(var_set, t + 1)
                nc.scalar.activation(std[:, :], mv[:, 1:2], ACT.Sqrt, bias=epsc[:, :]).then_inc(std_set, 1)
                act.wait_ge(aff_set, t + 1)
                o = a32[t % 2][:, :] if t < HT else h2[:, t - HT, :]
                if t < HT and t >= 2:
                    act.wait_ge(a1l_set, t - 1)
                if t == HT:
                    act.wait_ge(z_sum, HT)
                z0 = zbank(t, 0)
                n0 = CH[0][1]
                nc.scalar.activation(o[:, 0:n0], ps[:, z0, 0:n0], ACT.Relu, bias=col[:, 3:4],
                                     scale=col[:, 2:3]).then_inc(act_set, 1)
                nc.scalar.activation(o[:, n0:N].rearrange("p (b c) -> p b c", b=2),
                                     ps[:, z0 + 1:z0 + 3, 0:(N - n0) // 2], ACT.Relu, bias=col[:, 3:4],
                                     scale=col[:, 2:3]).then_inc(act_set, 1)

            def w2_high(t):
                act.wait_ge(z_sum, t + 1)
                if t == 0:
                    act.wait_ge(w2_in, 16)
                nc.scalar.activation(wh[:, t, :], w2s[:, t, :], ACT.Copy).then_inc(w2h_set, 1)

            def A_out(j):
                act.wait_ge(A_T, j + 1)
                if j >= len(stage):
                    act.wait_ge(spilled[j % len(stage)], 16 * (j // len(stage)))
                o, i = part_out(j)
                nc.scalar.activation(o, i, ACT.Copy).then_inc(A_act, 1)

            for j in range(0, JT, 2):
                A_out(j)
            for t in range(HT):
                affine(t)
                more = list(range((t + 1) * JT, min(NJ, (t + 2) * JT), 2))
                if more:
                    A_out(more[0])
                if t == 0:
                    act.wait_ge(h0_sum, NI)
                if t == HT // 2:
                    act.wait_ge(A_T, NJ)
                    act.wait_ge(deg_set, NT)
                act.wait_ge(act_set, 2 * t + 2)
                nc.scalar.activation(a1(a1h, t), a32[t % 2][:, :], ACT.Copy).then_inc(a1h_set, 1)
                for j in more[1:2]:
                    A_out(j)
                w2_high(t)
                for j in more[2:]:
                    A_out(j)
            act.wait_ge(lw_in, 32)
            act.wait_ge(lb1_in, 16)
            act.wait_ge(a1l_set, HT - 1)
            act.wait_ge(a1l_last, 1)
            nc.scalar.activation(lw1h[:, :, :], lws[:, :, :], ACT.Copy).then_inc(lwh_set, 1)
            nc.scalar.activation(lw2h[:, :, :], lw2s[:, :, :], ACT.Copy).then_inc(lwh_set, 1)
            nc.scalar.activation(lb1h[:, :], lb1r[:, :], ACT.Copy).then_inc(lwh_set, 1)
            for t in range(HT, BT):
                affine(t)

            def ln_root(k):
                act.wait_ge(ln_var, k + 1)
                r = rows[k]
                nc.scalar.activation(ln_std[0:r, k:k + 1], ln_mv[0:r, k, 1:2], ACT.Sqrt,
                                     bias=epsc[0:r, :]).then_inc(ln_std_s, 1)

            def ln_apply(k):
                act.wait_ge(ln_aff, k + 1)
                r = rows[k]
                nc.scalar.activation(xs[0:r, k, :], xs[0:r, k, :], ACT.Identity, bias=ln_r[0:r, k, 1:2],
                                     scale=ln_r[0:r, k, 0:1]).then_inc(x1_set, 1)

            def xt_high(k):
                r = rows[k]
                act.wait_ge(x1_T, k + 1)
                if k == 0:
                    act.wait_ge(lwl_set, 3)
                if k >= 2:
                    act.wait_ge(u_sum, k - 1)
                nc.scalar.activation(xth[:, k % 2, :].rearrange("p (d c) -> p d c", c=P)[:, :, 0:r],
                                     ps[:, 1, :].rearrange("p (d c) -> p d c", c=P)[:, :, 0:r],
                                     ACT.Copy).then_inc(xth_set, 1)

            def u_relu(k):
                r = rows[k]
                act.wait_ge(u_sum, k + 1)
                if k >= 2:
                    act.wait_ge(ul_set, k - 1)
                nc.scalar.activation(u32[0:r, k % 2, :], ps[0:r, 2, 0:L], ACT.Relu).then_inc(u32_set, 1)
                act.wait_ge(u32_set, k + 1)
                nc.scalar.activation(uh[0:r, k, :], u32[0:r, k % 2, :], ACT.Copy).then_inc(uh_set, 1)

            for s in range(NT + 2):
                if 0 <= s - 1 < NT:
                    xt_high(s - 1)
                if s < NT:
                    ln_root(s)
                    ln_apply(s)
                if 0 <= s - 2 < NT:
                    u_relu(s - 2)
            for i, b in enumerate(v_order):
                act.wait_ge(v_sum, i + 1)
                if i == 0:
                    act.wait_ge(u_sum, NT)
                f = slice(b * BANK, b * BANK + v_width[b])
                nc.scalar.activation(vh[:, f], ps[:, V0 + b, 0:v_width[b]], ACT.Copy).then_inc(vh_set, 1)

            sq = [u32[:, :, :].rearrange("p a b -> p (a b)"), lw1h[:, 0:2, :].rearrange("p a b -> p (a b)")]

            def ln2_root(k):
                act.wait_ge(ln2_mean, k + 1)
                if k == 0:
                    act.wait_ge(ul_set, NT)
                    act.wait_ge(u_sum, NT)
                r = rows[k]
                nc.scalar.activation(sq[k % 2][0:r, :], xs[0:r, k, :], ACT.Square, bias=ln_m[0:r, k, 1:2],
                                     accum_out=ln_q[0:r, k:k + 1]).then_inc(ln2_var, 1)
                act.wait_ge(ln2_var, k + 1)
                nc.scalar.activation(ln_std[0:r, k:k + 1], ln_q[0:r, k:k + 1], ACT.Sqrt,
                                     bias=epsc[0:r, :], scale=1.0 / D).then_inc(ln2_std, 1)

            def ln2_apply(k):
                act.wait_ge(ln2_aff, k + 1)
                r = rows[k]
                nc.scalar.activation(xs[0:r, k, :], xs[0:r, k, :], ACT.Identity, bias=ln_r[0:r, k, 1:2],
                                     scale=ln_r[0:r, k, 0:1]).then_inc(out_odd, 1)

            for s in range(NT + 1):
                if s < NT:
                    ln2_root(s)
                if s >= 1 and (s - 1) % 2:
                    ln2_apply(s - 1)

        @block.vector
        def _(v):
            n = [0]

            def link(ins):
                n[0] += 1
                ins.then_inc(dve, 1)
                v.wait_ge(dve, n[0])

            v.wait_ge(dst_in, 16)
            v.wait_ge(const, 3)
            link(nc.vector.tensor_copy(dst_f[0:ER, 0:EC], dst_i[0:ER, :]))
            v.wait_ge(prev_in, 16)
            link(nc.vector.tensor_copy(prev_f[0:ER, :], prev_i[0:ER, :]))
            link(nc.vector.tensor_scalar(after[0:ER, :], win_row[0:ER, :], prev_f[0:ER, 0:1], None, ALU.is_gt))
            link(nc.vector.tensor_scalar(below[0:ER, :], win_row[0:ER, :], dst_f[0:ER, EC - 1:EC], None, ALU.is_gt))
            nc.vector.tensor_tensor(edge_row[0:ER, :], after[0:ER, :], below[0:ER, :],
                                    ALU.subtract).then_inc(rowsel, 1)
            v.wait_ge(rowed, 1)
            link(nc.vector.tensor_scalar(less[0:NW, :], ps[0:NW, 2, 0:EC], win_col[0:NW, 0:1], 0.0, ALU.is_lt,
                                         ALU.add, accum_out=lo_n[0:NW, 0:1]))
            link(nc.vector.tensor_tensor(lo_n[0:NW, 1:2], lo_n[0:NW, 0:1], ps[0:NW, 2, EC:EC + 1], ALU.add))
            link(nc.vector.tensor_scalar(lo_n[0:NW, 2:3], lo_n[0:NW, 1:2], float(E - RUN), 0.0, ALU.min, ALU.max))
            nc.vector.tensor_copy(start_i[0:NW, :], lo_n[0:NW, 2:3]).then_inc(start_set, 1)
            v.wait_ge(eps_in_s, 16)
            v.wait_ge(ident_set, 1)
            link(nc.vector.tensor_scalar(eps1[:, :], eps_in[:, :], 1.0, None, ALU.add))
            link(nc.vector.tensor_scalar(diag[:, :], ident[:, :], eps1[:, 0:1], None, ALU.mult))
            link(nc.vector.tensor_copy(diag_h[:, :], diag[:, :]))
            nc.vector.tensor_tensor(diag_l[:, :], diag[:, :], diag_h[:, :].bitcast(F32),
                                    ALU.subtract).then_inc(diag_set, 1)
            v.wait_ge(par_T, 1)
            nc.vector.tensor_copy(par[:, :], ps[:, 4, 0:3 * BT]).then_inc(par_set, 1)
            v.wait_ge(run_d_in, 16)
            link(nc.vector.tensor_scalar(off[0:NW, :], run_d[0:NW, :], win_col[0:NW, 0:1], None, ALU.subtract))
            nc.vector.tensor_scalar(over[0:NW, :], off[0:NW, :], float(WIN), BIG, ALU.is_ge, ALU.mult).then_inc(dve, 1)
            n[0] += 1
            link(nc.vector.tensor_scalar(under[0:NW, :], off[0:NW, :], 0.0, BIG, ALU.is_lt, ALU.mult))
            link(nc.vector.tensor_tensor_reduce(out=outside[0:NW, :], in0=over[0:NW, :], in1=under[0:NW, :], scale=1.0,
                                                scalar=0.0, op0=ALU.add, op1=ALU.add, accum_out=n_out[0:NW, :]))
            v.wait_ge(run_s_in, 16)
            link(nc.vector.tensor_scalar(hi_i[0:NW, :], run_s[0:NW, :], 7, None, ALU.logical_shift_right))
            link(nc.vector.scalar_tensor_tensor(out=key0[0:NW, :], in0=hi_i[0:NW, :], scalar=float(WIN),
                                                in1=off[0:NW, :], op0=ALU.mult, op1=ALU.add))
            nc.vector.tensor_tensor(key[0:NW, :], key0[0:NW, :], outside[0:NW, :], ALU.add).then_inc(keys_set, 1)
            link(nc.vector.tensor_scalar(lo_i[0:NW, :], run_s[0:NW, :], P - 1, None, ALU.bitwise_and))
            nc.vector.tensor_copy(lo_f[0:NW, :], lo_i[0:NW, :]).then_inc(keys_set, 1)
            v.wait_ge(keys_T, 1)
            q = ps[:, 3, 0:4 * NW].rearrange("p (a c w) -> p a w c", a=2, c=2)
            link(nc.vector.tensor_copy(keyT[:, :, :], q[:, 0]))
            link(nc.vector.tensor_copy(loT[:, :, :], q[:, 1]))
            v.wait_ge(counted, 1)
            nc.vector.tensor_scalar(flag[0:1, :], ps[0:1, 5, 0:1], BIG * (NW * RUN - E), None,
                                    ALU.not_equal).then_inc(flag_set, 1)

            def one_hots(g):
                if g >= 2:
                    v.wait_ge(built, g - 1)
                w = slice(g * WG, (g + 1) * WG)
                nc.vector.tensor_tensor(
                    hot_s[g % 2][:, :, :, :], iota2[:, None, :, :].broadcast_to([P, WG, P, 2]),
                    loT[:, w, None, :].broadcast_to([P, WG, P, 2]), ALU.is_equal).then_inc(hot, 1)
                nc.vector.tensor_tensor(
                    hot_k[g % 2][:, :, :, :], iota2[:, None, 0:KEYS, :].broadcast_to([P, WG, KEYS, 2]),
                    keyT[:, w, None, :].broadcast_to([P, WG, KEYS, 2]), ALU.is_equal).then_inc(hot, 1)

            def h0_low(i):
                c, d = divmod(i, DT)
                c0, c1 = CH[c]
                v.wait_ge(h0h_set, i + 1)
                nc.vector.tensor_tensor(h0l[:, d, c0:c1], ps[:, 2 + i % 6, 0:c1 - c0],
                                        h0h[:, d, c0:c1].bitcast(F32), ALU.subtract).then_inc(h0l_set, 1)

            v.wait_ge(flag_set, 1)
            bad = v.value_load(flag[0:1, 0:1], min_val=0, max_val=1)
            with v.If(bad == 0):
                late = []
                for g in range(NG):
                    one_hots(g)
                    while late and late[0][0] <= g:
                        h0_low(late.pop(0)[1])
                    late += [(g + 2, i) for i in items_after[g]]
                for _, i in late:
                    h0_low(i)
            with v.Else():
                v.wait_ge(src_in, 16)
                v.wait_ge(const, 9)
                nc.vector.tensor_copy(gen_src[0:ER, :], src_i[0:ER, :]).then_inc(gen_copied, 1)
                with v.Fori(0, NT) as h:
                    with v.Fori(0, EC) as f:
                        v.wait_ge(gen_copied, h * 4 + 1)
                        v.wait_ge(gen_used, h * (EC + 1) + f + 1)
                        nc.vector.tensor_scalar(gen_s[0:ER, :], iota2[0:ER, :, 0], gen_src[0:ER, bass.ds(f, 1)],
                                                None, ALU.is_equal).then_inc(gen_hot, 1)
                        nc.vector.tensor_scalar(gen_d[0:ER, :], nodes[0:ER, :], dst_f[0:ER, bass.ds(f, 1)],
                                                None, ALU.is_equal).then_inc(gen_hot, 1)
                    v.wait_ge(gen_sum, h + 1)
                    for c, (c0, c1) in enumerate(CH):
                        nc.vector.tensor_copy(AT[:, bass.ds(h, 1), c0:c1],
                                              ps[:, 2 + c, None, 0:c1 - c0]).then_inc(gen_copied, 1)
                    nc.vector.tensor_scalar(gen_src[0:ER, :], gen_src[0:ER, :], -float(P), None,
                                            ALU.add).then_inc(gen_copied, 1)
                v.wait_ge(gen_copied, 4 * NT + 1)
                nc.vector.memset(n_out[:, :], 0.0).then_inc(AT_set, NG)
                for i in range(NI - DT):
                    h0_low(i)
            for i in range(NI - DT, NI):
                h0_low(i)

            def batch_norm(t):
                if t < BT - 1:
                    v.wait_ge(z_sum, t + 1)
                if t == 0:
                    v.wait_ge(par_set, 1)
                i = t if t < HT else t + 2 * HT
                step = HT if t < HT else DT
                b, g, be = (par[:, i + j * step:i + j * step + 1] for j in range(3))
                for c, (c0, c1) in enumerate(CH):
                    if t == BT - 1:
                        v.wait_ge(z_part, c + 1)
                    link(nc.vector.bn_stats(stats[:, 6 * c:6 * c + 6], ps[:, zbank(t, c), 0:c1 - c0]))
                nc.vector.bn_aggr(mv[:, :], stats[:, :]).then_inc(var_set, 1)
                v.wait_ge(var_set, t + 1)
                link(nc.vector.tensor_tensor(col[:, 0:1], mv[:, 0:1], b, ALU.add))
                link(nc.vector.tensor_tensor(col[:, 1:2], b, col[:, 0:1], ALU.subtract))
                v.wait_ge(std_set, t + 1)
                link(nc.vector.reciprocal(rstd[:, :], std[:, :]))
                if t >= 1:
                    v.wait_ge(act_set, 2 * t)
                link(nc.vector.tensor_tensor(col[:, 2:3], rstd[:, :], g, ALU.mult))
                nc.vector.scalar_tensor_tensor(out=col[:, 3:4], in0=col[:, 1:2], scalar=col[:, 2:3], in1=be,
                                               op0=ALU.mult, op1=ALU.add).then_inc(aff_set, 1)

            def A_out(j):
                v.wait_ge(A_T, j + 1)
                if j >= len(stage):
                    v.wait_ge(spilled[j % len(stage)], 16 * (j // len(stage)))
                o, i = part_out(j)
                nc.vector.tensor_copy(o, i).then_inc(A_dve, 1)

            v.wait_ge(loops_set, NT)
            def degree(k):
                nc.vector.tensor_reduce(deg1[:, k:k + 1], AT[:, k, :].bitcast(F32), AX_X, ALU.add).then_inc(deg_set, 1)

            todo = list(range(NT))
            for t in range(-1, HT):
                if t >= 0:
                    batch_norm(t)
                for j in range((t + 1) * JT + 1, min(NJ, (t + 2) * JT), 2):
                    A_out(j)
                    if todo and t < HT // 2 and j % JT < (JT - 1 if t >= 0 else JT):
                        degree(todo.pop(0))
            assert not todo
            v.wait_ge(a1h_set, HT)
            nc.vector.tensor_tensor(a1(a1l, HT - 1), a32[(HT - 1) % 2][:, :], a1(a1h, HT - 1).bitcast(F32),
                                    ALU.subtract).then_inc(a1l_last, 1)
            for t in range(HT, BT):
                batch_norm(t)

            def ln_stats(k):
                r = rows[k]
                v.wait_ge(h2_T, k + 1)
                link(nc.vector.scalar_tensor_tensor(out=xs[0:r, k, :], in0=xs[0:r, k, :], scalar=2.0,
                                                    in1=ps[0:r, 0, :], op0=ALU.mult, op1=ALU.add))
                link(nc.vector.bn_stats(ln_s[0:r, k, :], xs[0:r, k, :]))
                nc.vector.bn_aggr(ln_mv[0:r, k, :], ln_s[0:r, k, :]).then_inc(ln_var, 1)

            def ln_scale(k, root, done):
                r = rows[k]
                v.wait_ge(root, k + 1)
                link(nc.vector.reciprocal(ln_r[0:r, k, 0:1], ln_std[0:r, k:k + 1]))
                nc.vector.scalar_tensor_tensor(out=ln_r[0:r, k, 1:2], in0=ln_mv[0:r, k, 0:1], scalar=-1.0,
                                               in1=ln_r[0:r, k, 0:1], op0=ALU.mult, op1=ALU.mult).then_inc(done, 1)

            def xt_low(k):
                r = rows[k]
                v.wait_ge(xth_set, k + 1)
                nc.vector.tensor_tensor(xtl[:, k % 2, :].rearrange("p (d c) -> p d c", c=P)[:, :, 0:r],
                                        ps[:, 1, :].rearrange("p (d c) -> p d c", c=P)[:, :, 0:r],
                                        xth[:, k % 2, :].rearrange("p (d c) -> p d c", c=P)[:, :, 0:r].bitcast(F32),
                                        ALU.subtract).then_inc(xtl_set, 1)

            v.wait_ge(x_again, 32)
            for s in range(NT + 1):
                if s < NT:
                    ln_stats(s)
                    ln_scale(s, ln_std_s, ln_aff)
                if s >= 1:
                    xt_low(s - 1)

            def base(k):
                r = rows[k]
                v.wait_ge(x1_T, k + 1)
                nc.vector.scalar_tensor_tensor(out=xs[0:r, k, :], in0=b2_all[0:r, :], scalar=deg1[0:r, k:k + 1],
                                               in1=xs[0:r, k, :], op0=ALU.mult, op1=ALU.add).then_inc(base_set, 1)

            v.wait_ge(b2_in, 16)
            v.wait_ge(deg_set, NT)
            for k in range(NT):
                base(k)
            for i, b in enumerate(v_order):
                v.wait_ge(vh_set, i + 1)
                f = slice(b * BANK, b * BANK + v_width[b])
                nc.vector.tensor_tensor(vl[:, f], ps[:, V0 + b, 0:v_width[b]], vh[:, f].bitcast(F32),
                                        ALU.subtract).then_inc(vl_set, 1)

            def ln2_sum(k):
                r = rows[k]
                v.wait_ge(y_sum, k + 1)
                link(nc.vector.tensor_tensor_reduce(out=xs[0:r, k, :], in0=ps[0:r, k % V0, :], in1=xs[0:r, k, :],
                                                    scale=1.0, scalar=0.0, op0=ALU.add, op1=ALU.add,
                                                    accum_out=ln_m[0:r, k, 0:1]))
                nc.vector.tensor_scalar(ln_m[0:r, k, 1:2], ln_m[0:r, k, 0:1], -1.0 / D, None,
                                        ALU.mult).then_inc(ln2_mean, 1)

            def ln2_scale(k):
                r = rows[k]
                v.wait_ge(ln2_std, k + 1)
                link(nc.vector.reciprocal(ln_r[0:r, k, 0:1], ln_std[0:r, k:k + 1]))
                nc.vector.tensor_tensor(ln_r[0:r, k, 1:2], ln_m[0:r, k, 1:2], ln_r[0:r, k, 0:1],
                                        ALU.mult).then_inc(ln2_aff, 1)

            v.wait_ge(base_set, NT)
            for s in range(NT + 1):
                if s < NT:
                    ln2_sum(s)
                if s >= 1:
                    ln2_scale(s - 1)

        @block.tensor
        def _(pe):
            mm = nc.tensor.matmul
            pe.wait_ge(rowsel, 1)
            mm(ps[0:NW, 2, 0:EC], edge_row[0:ER, :], dst_f[0:ER, 0:EC], start=True, stop=True)
            mm(ps[0:NW, 2, EC:EC + 1], below[0:ER, :], dst_f[0:ER, EC:EC + 1], start=True, stop=True).then_inc(rowed, 1)
            pe.wait_ge(ident_set, 1)
            pe.wait_ge(par_in, 6 * 16)
            nc.tensor.transpose(ps[:, 4, 0:3 * BT], par_r[0:3 * BT, :], ident[0:3 * BT, 0:3 * BT]).then_inc(par_T, 1)
            pe.wait_ge(keys_set, 2)
            for a, s in enumerate((key, lo_f)):
                for c in range(2):
                    o = (2 * a + c) * NW
                    last = nc.tensor.transpose(ps[:, 3, o:o + NW], s[0:NW, c * P:c * P + P], ident[0:NW, 0:NW])
            last.then_inc(keys_T, 1)
            pe.wait_ge(const, 9)
            mm(ps[0:1, 5, 0:1], n_out[0:NW, :], ones[0:NW, :], start=True, stop=True).then_inc(counted, 1)

            def build(g):
                pe.wait_ge(hot, 2 * g + 2)
                if g >= 2:
                    pe.wait_ge(AT_set, g - 1)
                for w in range(WG):
                    for c in range(2):
                        last = mm(ps[:, g % 2, w * KEYS:(w + 1) * KEYS], hot_s[g % 2][:, w, :, c],
                                  hot_k[g % 2][:, w, :, c], start=(c == 0), stop=(c == 1))
                last.then_inc(built, 1)

            def aggregate(i, k):
                c, d = divmod(i, DT)
                c0, c1 = CH[c]
                r = rows[k]
                o = ps[:, 2 + i % 6, 0:c1 - c0]
                if k == 0:
                    pe.wait_ge(AT_set, CHG[c])
                    if i == 0:
                        pe.wait_ge(diag_set, 1)
                    if i >= 6:
                        pe.wait_ge(h0l_set, i - 5)
                if i == 0:
                    pe.wait_ge(xl_set, k + 1)
                ds = slice(d * P, d * P + P)
                a, b = max(c0, P * k), min(c1, P * k + r)
                parts = [(xh, AT[0:r, k, c0:c1], o), (xl, AT[0:r, k, c0:c1], o)]
                if a < b:
                    dc = slice(a - P * k, b - P * k)
                    oo = ps[:, 2 + i % 6, a - c0:b - c0]
                    parts += [(xh, diag_h[0:r, dc], oo), (xl, diag_h[0:r, dc], oo), (xh, diag_l[0:r, dc], oo)]
                for j, (part, rhs, oo) in enumerate(parts):
                    last = mm(oo, part[0:r, k, ds], rhs, start=(k == 0 and j == 0),
                              stop=(k == NT - 1 and j == len(parts) - 1), skip_group_check=True)
                if k == NT - 1:
                    last.then_inc(h0_sum, 1)

            pe.wait_ge(flag_set, 1)
            bad = pe.value_load(flag[0:1, 0:1], min_val=0, max_val=1)
            with pe.If(bad == 0):
                for g in range(NG):
                    build(g)
                    for u in slot_units[g]:
                        aggregate(*u)
            with pe.Else():
                with pe.Fori(0, NT) as h:
                    pe.wait_ge(gen_copied, h * 4 + 1)
                    for c, (c0, c1) in enumerate(CH):
                        last = mm(ps[:, 2 + c, 0:c1 - c0], gen_0[0:ER, 0:P], gen_0[0:ER, 0:c1 - c0], start=True,
                                  stop=False, skip_group_check=True)
                    last.then_inc(gen_used, 1)
                    with pe.Fori(0, EC) as f:
                        pe.wait_ge(gen_hot, (h * EC + f) * 2 + 2)
                        for c, (c0, c1) in enumerate(CH):
                            last = mm(ps[:, 2 + c, 0:c1 - c0], gen_s[0:ER, :], gen_d[0:ER, c0:c1], start=False,
                                      stop=False, skip_group_check=True)
                        last.then_inc(gen_used, 1)
                    for c, (c0, c1) in enumerate(CH):
                        last = mm(ps[:, 2 + c, 0:c1 - c0], gen_0[0:ER, 0:P], gen_0[0:ER, 0:c1 - c0], start=False,
                                  stop=True, skip_group_check=True)
                    last.then_inc(gen_sum, 1)
                for u in units[0:(len(CH) - 1) * per]:
                    aggregate(*u)
            for u in tail_units:
                aggregate(*u)

            def A_rows(j):
                kd, q = divmod(j, AQ)
                pe.wait_ge(loops_set, kd + 1)
                if j >= 2:
                    pe.wait_ge((A_act, A_dve)[j % 2], j // 2)
                for ks in range(4 * q, min(NT, 4 * q + 4)):
                    o = (ks - 4 * q) * P
                    last = nc.tensor.transpose(ps[0:rows[kd], j % 2, o:o + rows[ks]],
                                               AT[0:rows[ks], ks, P * kd:P * kd + rows[kd]].bitcast(F32),
                                               ident[0:rows[ks], 0:rows[ks]])
                last.then_inc(A_T, 1)

            pe.wait_ge(w1l_set, DT)
            pair_at = [(1, DT - 1), (2, DT // 2 - 1), (2, DT - 1)]
            for t in range(HT):
                if t >= 2:
                    pe.wait_ge(act_set, 2 * t - 2)
                for c, (c0, c1) in enumerate(CH):
                    if t == 0:
                        pe.wait_ge(h0l_set, max(DT * (c + 1), 7 + c))
                    for d in range(DT):
                        for j, (w, h) in enumerate(((wh, h0h), (wl, h0h), (wh, h0l))):
                            last = mm(ps[:, zbank(t, c), 0:c1 - c0], w[:, t, d * P:d * P + P], h[:, d, c0:c1],
                                      start=(d == 0 and j == 0), stop=(d == DT - 1 and j == 2))
                        if c == len(CH) - 1 and d == DT - 1:
                            last.then_inc(z_sum, 1)
                        if (c, d) in pair_at:
                            j0 = t * JT + 2 * pair_at.index((c, d))
                            for j in range(j0, min(NJ, j0 + 2)):
                                A_rows(j)

            half = HT // 2
            runs = [(t, 0, HT) for t in range(HT, BT - 2)]
            runs += [(t, k0, k0 + half) for k0 in (0, half) for t in (BT - 2, BT - 1)]

            def hidden2(t, k, j, c):
                w, a = ((wh, a1h), (wl, a1h), (wh, a1l))[j]
                c0, c1 = CH[c]
                return mm(ps[:, zbank(t, c), 0:c1 - c0], w[:, k, (t - HT) * P:(t - HT + 1) * P], a1(a, k)[:, c0:c1],
                          start=(k == 0 and j == 0), stop=(k == HT - 1 and j == 2))

            for t, k0, k1 in runs:
                if k0 == 0:
                    pe.wait_ge(act_set, 2 * t - 2)
                for k in range(k0, k1):
                    if t == HT:
                        pe.wait_ge(w2l_set, k + 1)
                        if k < HT - 1:
                            pe.wait_ge(a1l_set, k + 1)
                        else:
                            pe.wait_ge(a1l_last, 1)
                    if (t, k1) != (BT - 1, HT):
                        for j in range(3):
                            for c in range(len(CH)):
                                last = hidden2(t, k, j, c)
                if (t, k1) == (BT - 1, HT):
                    for c in range(len(CH)):
                        for k in range(k0, k1):
                            for j in range(3):
                                last = hidden2(t, k, j, c)
                        last.then_inc(z_part, 1)
                elif k1 == HT:
                    last.then_inc(z_sum, 1)
                elif t == BT - 1:
                    last.then_inc(a1_first_used, 1)

            def h2_rows(k):
                r = rows[k]
                if k < 2:
                    assert CH[0][1] >= P
                    pe.wait_ge(act_set, 2 * BT - 1 + k)
                if k >= 1:
                    pe.wait_ge(ln_var, k)
                for m in range(DT):
                    last = nc.tensor.transpose(ps[0:r, 0, m * P:m * P + P], h2[:, m, P * k:P * k + r], ident[:, :])
                last.then_inc(h2_T, 1)

            def x1_cols(k):
                r = rows[k]
                pe.wait_ge(x1_set, k + 1)
                if k >= 1:
                    pe.wait_ge(xtl_set, k)
                for d in range(DT):
                    last = nc.tensor.transpose(ps[:, 1, d * P:d * P + r], xs[0:r, k, d * P:d * P + P],
                                               ident[0:r, 0:r])
                last.then_inc(x1_T, 1)

            def hidden(k):
                r = rows[k]
                pe.wait_ge(xtl_set, k + 1)
                if k == 0:
                    pe.wait_ge(lwl_set, 3)
                if k >= 1:
                    pe.wait_ge(u32_set, k)
                o = ps[0:r, 2, 0:L]
                mm(o, one_r[:, 0:r], lb1h[:, :], start=True, stop=False)
                mm(o, one_r[:, 0:r], lb1l[:, :], start=False, stop=False)
                for d in range(DT):
                    for j, (xt, w) in enumerate(((xth, lw1h), (xtl, lw1h), (xth, lw1l))):
                        last = mm(o, xt[:, k % 2, d * P:d * P + r], w[:, d, :], start=False,
                                  stop=(d == DT - 1 and j == 2))
                last.then_inc(u_sum, 1)

            def own_and_neighbours(k):
                r = rows[k]
                pe.wait_ge(ul_set, k + 1)
                pe.wait_ge(A_in[k // 2], 16 if rows[k - k % 2 + 1] == P else 32)

                def product(m, j, b, c0, c1):
                    f = m * N - b * BANK
                    return mm(ps[:, V0 + b, f + c0:f + c1], (uh, ul)[j][0:r, k, m * P:m * P + P], a_rows(k)[0:r, c0:c1],
                              start=(k == 0 and j == 0 and v_first[b] == m), stop=(k == NT - 1 and j == 1),
                              skip_group_check=True)

                if k < NT - 1:
                    for m in range(LT):
                        for j in range(2):
                            for mb, b, c0, c1 in v_blocks:
                                if mb == m:
                                    product(m, j, b, c0, c1)
                    return
                for bank in v_order:
                    for m, b, c0, c1 in v_blocks:
                        if b == bank:
                            for j in range(2):
                                last = product(m, j, b, c0, c1)
                    last.then_inc(v_sum, 1)

            for s in range(-1, NT + 3):
                if 0 <= s - 1 < NT:
                    x1_cols(s - 1)
                if 0 <= s - 2 < NT:
                    hidden(s - 2)
                if s + 1 < NT:
                    h2_rows(s + 1)
                if s >= 3:
                    own_and_neighbours(s - 3)

            for k in range(NT):
                r = rows[k]
                pe.wait_ge(vl_set, v_needed(k))
                if k >= V0:
                    pe.wait_ge(ln2_mean, k - V0 + 1)
                for m in range(LT):
                    f = m * N + P * k
                    for j, (part, w) in enumerate(((vh, lw2h), (vl, lw2h), (vh, lw2l))):
                        last = mm(ps[0:r, k % V0, :], part[:, f:f + r], w[:, m, :],
                                  start=(m == 0 and j == 0), stop=(m == LT - 1 and j == 2))
                last.then_inc(y_sum, 1)


_INS = ["x", "src", "dst", "L0_gnn_eps", "L0_gnn_W1", "L0_gnn_b1", "L0_gnn_g1", "L0_gnn_be1", "L0_gnn_W2",
        "L0_gnn_b2", "L0_gnn_g2", "L0_gnn_be2", "L1_gnn_W1", "L1_gnn_b1", "L1_gnn_W2", "L1_gnn_b2"]


def kernel(**inputs):
    import numpy as np
    import concourse.bacc as bacc
    from concourse.bass_utils import run_bass_kernel_spmd

    nc = bacc.Bacc("TRN2", target_bir_lowering=False, num_devices=1)
    arrays, args = {}, []
    for name in _INS:
        a = np.ascontiguousarray(inputs[name]).reshape(np.shape(inputs[name]) or (1,))
        arrays[f"in_{name}"] = a
        args.append(nc.dram_tensor(f"in_{name}", a.shape, mybir.dt.from_np(a.dtype), kind="ExternalInput").ap())
    n, d = inputs["x"].shape
    args.append(nc.dram_tensor("out_0", (n, d), F32, kind="ExternalOutput").ap())
    args.append(nc.dram_tensor("a_spill", (n, n), F32, kind="Internal").ap())
    gnn_kernel(nc, *args)
    r = run_bass_kernel_spmd(nc, [arrays], core_ids=[0])
    return r.results[0]["out_0"]
```

```python
from contextlib import ExitStack

import concourse.bass as bass
from concourse import mybir
from concourse.alu_op_type import AluOpType as ALU

F32 = mybir.dt.float32
F32R = mybir.dt.float32r
BF16 = mybir.dt.bfloat16
I32 = mybir.dt.int32
ACT = mybir.ActivationFunctionType
AX_X = mybir.AxisListType.X

P = 128
EPS = 1e-5
BANK = 512


def cdiv(a, b):
    return -(-a // b)


def gnn_kernel(nc, x, src, dst, eps, w1, b1, g1, be1, w2, b2, g2, be2, lw1, lb1, lw2, lb2, out, a_spill):
    N, D = x.shape
    (E,) = src.shape
    H = w1.shape[1]
    L = lw1.shape[1]
    NT = cdiv(N, P)
    rows = [min(P, N - P * k) for k in range(NT)]
    DT, HT, LT = D // P, H // P, L // P
    WIN = 10
    NW = N // WIN
    RUN = 2 * P
    WG = 5
    NG = NW // WG
    KEYS = NT * WIN
    GCOLS = WG * KEYS
    ER = NW
    EC = E // ER
    assert N % WIN == 0 and NW % WG == 0 and E % ER == 0 and GCOLS <= BANK and NW <= P
    CH = [(0, 250), (250, 750), (750, 1250)]
    CHG = [5, 15, 25]
    assert CH[-1][1] == N and all(g * WG * WIN == c[1] for g, c in zip(CHG, CH))
    last_order = [1, 2, 0]
    BT = HT + DT

    ctx = ExitStack()
    with ctx:
        def sem(name):
            return ctx.enter_context(nc.semaphore(name))

        base = cdiv(nc.sbuf_base, 64) * 64
        KB = 1024
        R_X, R_X2, R_AT = base, base + 20 * KB, base + 60 * KB
        R_H0 = R_AT + cdiv(NT * N * 4, 64) * 64
        R_W1S = R_H0 + 2 * DT * CH[-1][0] * 4
        R_W = R_W1S + DT * H * 4
        assert R_W >= R_H0 + 2 * DT * N * 4
        R_HOT = R_W + 32 * KB
        R_MISC = R_HOT + 2 * cdiv(N * 4, 64) * 64
        cursor = [R_MISC]

        def at(name, shape, dt, offset):
            return nc.alloc_sbuf_tensor_at(name, shape, dt, offset=offset)

        def misc(name, shape, dt):
            n = 4 if dt != BF16 else 2
            for s in shape[1:]:
                n *= s
            o = cursor[0]
            cursor[0] += cdiv(n, 32) * 32
            return at(name, shape, dt, o)

        xs = at("xs", [P, NT, D], F32, R_X)
        w1s = at("w1s", [P, DT, H], F32, R_W1S)
        w2s = at("w2s", [P, HT, D], F32, R_X)
        xh = at("xh", [P, NT, D], F32R, R_X2)
        xl = at("xl", [P, NT, D], F32R, R_X2 + 20 * KB)
        AT = at("AT", [P, NT, N], F32R, R_AT)
        h0h = [at(f"h0h{c}", [P, DT, c1 - c0], F32R, R_H0 + 2 * DT * c0 * 4) for c, (c0, c1) in enumerate(CH)]
        h0l = [at(f"h0l{c}", [P, DT, c1 - c0], F32R, R_H0 + DT * (c0 + c1) * 4) for c, (c0, c1) in enumerate(CH)]
        wh = at("wh", [P, HT, DT * P], F32R, R_W)
        wl = at("wl", [P, HT, DT * P], F32R, R_W + 16 * KB)
        hot_s = [at(f"hot_s{i}", [P, WG, P, 2], BF16, R_HOT + i * 4608) for i in range(2)]
        hot_k = [at(f"hot_k{i}", [P, WG, KEYS, 2], BF16, R_HOT + i * 4608 + 2560) for i in range(2)]
        a1h = [at(f"a1h{i}", [P, HT // 2, N], F32R, (R_X2, R_AT)[i]) for i in range(2)]
        a1l = [at(f"a1l{i}", [P, HT // 2, N], F32R, (R_X2, R_AT)[i] + 2 * N * HT) for i in range(2)]
        a32 = [at(f"a32_{i}", [P, N], F32, R_HOT + i * cdiv(N * 4, 64) * 64) for i in range(2)]
        h2 = at("h2", [P, DT, N], F32, R_H0)
        lws = at("lws", [P, DT, L], F32, R_H0 + DT * N * 4)
        lw2s = at("lw2s", [P, LT, D], F32, R_H0 + DT * N * 4 + 4 * KB)
        lw2h = at("lw2h", [P, LT, D], F32R, R_H0 + DT * N * 4 + 8 * KB)
        lw2l = at("lw2l", [P, LT, D], F32R, R_H0 + DT * N * 4 + 12 * KB)
        lw1h = at("lw1h", [P, DT, L], F32R, R_HOT)
        lw1l = at("lw1l", [P, DT, L], F32R, R_HOT + 4 * KB)
        A = [at("A0", [P, 8, N], F32R, R_X2), at("A1", [P, NT - 8, N], F32R, R_AT)]
        uh = at("uh", [P, NT, L], F32R, R_W)
        ul = at("ul", [P, NT, L], F32R, R_W + 10 * KB)
        vh = at("vh", [P, LT * N], F32R, R_H0)
        vl = at("vl", [P, LT * N], F32R, R_H0 + cdiv(LT * N * 4, 64) * 64)
        nodes = at("nodes", [P, N], F32, R_H0)
        gen_src = at("gen_src", [P, EC], F32, R_H0 + 5 * KB)
        gen_s = at("gen_s", [P, P], BF16, R_H0 + 6 * KB)
        gen_d = at("gen_d", [P, N], BF16, R_H0 + 7 * KB)
        gen_0 = at("gen_0", [P, BANK], BF16, R_H0 + 10 * KB)
        TMP = [R_W]

        def tmp(name, shape, dt):
            o = TMP[0]
            TMP[0] += cdiv(shape[1] * 4, 32) * 32
            return at(name, shape, dt, o)

        dst_i = tmp("dst_i", [P, EC], I32)
        src_i = tmp("src_i", [P, EC], I32)
        dst_f = tmp("dst_f", [P, EC + 1], F32)
        prev_i = tmp("prev_i", [P, 1], I32)
        prev_f = tmp("prev_f", [P, 1], F32)
        win_row = tmp("win_row", [P, NW], F32)
        after = tmp("after", [P, NW], F32)
        below = tmp("below", [P, NW], F32)
        edge_row = tmp("edge_row", [P, NW], F32)
        less = tmp("less", [P, EC], F32)
        lo_n = tmp("lo_n", [P, 3], F32)
        start_i = tmp("start_i", [P, 1], I32)
        run_d = tmp("run_d", [P, RUN], I32)
        run_s = tmp("run_s", [P, RUN], I32)
        off = tmp("off", [P, RUN], F32)
        over = tmp("over", [P, RUN], F32)
        under = tmp("under", [P, RUN], F32)
        outside = tmp("outside", [P, RUN], F32)
        hi_i = tmp("hi_i", [P, RUN], I32)
        lo_i = tmp("lo_i", [P, RUN], I32)
        lo_f = tmp("lo_f", [P, RUN], F32)
        key = tmp("key", [P, RUN], F32)
        n_out = tmp("n_out", [P, 1], F32)
        par_r = tmp("par_r", [P, P], F32)

        ident = misc("ident", [P, P], F32)
        iota2 = misc("iota2", [P, P, 2], BF16)
        keyT = misc("keyT", [P, NW, 2], BF16)
        loT = misc("loT", [P, NW, 2], BF16)
        win_col = misc("win_col", [P, 1], F32)
        ones = misc("ones", [P, 1], F32)
        one_r = misc("one_r", [33, P], F32R)
        flag = misc("flag", [1, 1], I32)
        eps_in = misc("eps_in", [P, 1], F32)
        asked = misc("asked", [1, 1], F32)
        eps1 = misc("eps1", [P, 1], F32)
        diag = misc("diag", [P, P], F32)
        epsc = misc("epsc", [P, 1], F32)
        par = misc("par", [P, 3 * BT], F32)
        lb1r = misc("lb1r", [33, L], F32)
        lb1p = misc("lb1p", [33, L], F32R)
        b2_all = misc("b2_all", [P, D], F32)
        deg1 = misc("deg1", [P, NT], F32)
        stats = misc("stats", [P, 18], F32)
        mv = misc("mv", [P, 2], F32)
        std = misc("std", [P, 1], F32)
        rstd = misc("rstd", [P, 1], F32)
        col = misc("col", [P, 4], F32)
        ln_s = misc("ln_s", [P, NT, 6], F32)
        ln_mv = misc("ln_mv", [P, NT, 2], F32)
        ln_m = misc("ln_m", [P, NT, 2], F32)
        ln_q = misc("ln_q", [P, NT], F32)
        ln_std = misc("ln_std", [P, NT], F32)
        ln_r = misc("ln_r", [P, NT, 2], F32)
        u32 = misc("u32", [P, 2, L], F32)
        xth = at("xth", [P, 2, D], F32R, R_H0 + DT * N * 4)
        xtl = at("xtl", [P, 2, D], F32R, R_H0 + DT * N * 4 + 4 * KB)
        stage = [at(f"stage{i}", [P, BANK], F32, R_X + (16 + 2 * i) * KB) for i in range(2)]
        stage += [u32[:, :, :].rearrange("p a b -> p (a b)")]
        stage += [misc(f"stage{i}", [P, BANK], F32) for i in range(3, 5)]
        assert cursor[0] <= nc.sbuf_usable_end, (cursor[0], nc.sbuf_usable_end)

        ps = ctx.enter_context(nc.psum_tensor("ps", [P, 8, BANK], F32))

        dst_in, prev_in, src_in, eps_in_s, par_in, lb1_in, b2_in = (
            sem(n) for n in ("dst_in", "prev_in", "src_in", "eps_in_s", "par_in", "lb1_in", "b2_in"))
        x_in, x_in2, w1_in, w2_in, lw_in, x_again = (sem(n) for n in ("x_in", "x_in2", "w1_in", "w2_in", "lw_in", "x_again"))
        stored = sem("stored")
        spilled = [sem(f"spilled{i}") for i in range(len(stage))]
        A_in = [sem(f"A_in{i}") for i in range(cdiv(NT, 2))]
        runs_asked, lb1_zero = sem("runs_asked"), sem("lb1_zero")
        prev_set, const, ident_set = sem("prev_set"), sem("const"), sem("ident_set")
        dve = sem("dve")
        pool = sem("pool")
        rowsel, rowed, start_set, run_d_in, run_s_in = (
            sem(n) for n in ("rowsel", "rowed", "start_set", "run_d_in", "run_s_in"))
        keys_set, keys_T, n_out_set, counted, flag_set, par_T, par_set, diag_set = (
            sem(n) for n in ("keys_set", "keys_T", "n_out_set", "counted", "flag_set", "par_T", "par_set", "diag_set"))
        xh_set, xl_set, w1h_set, w1l_set = (sem(n) for n in ("xh_set", "xl_set", "w1h_set", "w1l_set"))
        hot, built, AT_set = sem("hot"), sem("built"), sem("AT_set")
        gen_hot, gen_used, gen_sum, gen_copied = (
            sem(n) for n in ("gen_hot", "gen_used", "gen_sum", "gen_copied"))
        h0_sum, h0h_set, h0l_set = sem("h0_sum"), sem("h0h_set"), sem("h0l_set")
        z_sum, z_part, var_set, std_set, aff_set, act_set = (
            sem(n) for n in ("z_sum", "z_part", "var_set", "std_set", "aff_set", "act_set"))
        a1h_set, a1l_set, a1l_last, w2h_set, w2l_set, deg_set = (
            sem(n) for n in ("a1h_set", "a1l_set", "a1l_last", "w2h_set", "w2l_set", "deg_set"))
        lwh_set, lwl_set = sem("lwh_set"), sem("lwl_set")
        h2_T, h2_used, ln_var, ln_std_s, ln_aff, x1_set, x1_T, xth_set, xtl_set = (
            sem(n) for n in ("h2_T", "h2_used", "ln_var", "ln_std_s", "ln_aff", "x1_set", "x1_T", "xth_set", "xtl_set"))
        u_sum, u32_set, uh_set, ul_set = (sem(n) for n in ("u_sum", "u32_set", "uh_set", "ul_set"))
        late_T, late_set = sem("late_T"), sem("late_set")
        loops_set, A_T, A_act, A_dve, a1_first_used = (
            sem(n) for n in ("loops_set", "A_T", "A_act", "A_dve", "a1_first_used"))
        v_sum, vh_set, vl_set, base_set = sem("v_sum"), sem("vh_set"), sem("vl_set"), sem("base_set")
        y_sum, ln2_mean, ln2_var, ln2_std, ln2_aff, out_pool, out_act, out_dve = (
            sem(n) for n in ("y_sum", "ln2_mean", "ln2_var", "ln2_std", "ln2_aff", "out_pool", "out_act", "out_dve"))

        full = P * (N // P)
        half = NT // 2
        RING = 6

        def zbank(t, n):
            return 2 + 3 * (t % 2) + n

        def a1(part, kt):
            return part[kt // (HT // 2)][:, kt % (HT // 2), :]

        def a_rows(k):
            return A[0][:, k, :] if k < 8 else A[1][:, k - 8, :]

        AQ = N // BANK
        LATE = AQ * BANK // P
        W_LATE = N - P * LATE
        NJ = NT * AQ
        JT = 4
        assert NJ // JT == HT // 2 + 1 and NJ % JT == 0 and NJ % len(stage) == 0 and LATE == HT and NT % 2 == 0

        VB = cdiv(LT * N, BANK)
        V0 = 8 - VB
        v_width = [min(BANK, LT * N - BANK * b) for b in range(VB)]
        v_blocks = [(m, b, max(0, b * BANK - m * N), min(N, (b + 1) * BANK - m * N))
                    for m in range(LT) for b in range(m * N // BANK, ((m + 1) * N - 1) // BANK + 1)]
        v_first = {b: m for m, b, _, _ in reversed(v_blocks)}
        v_order = []
        for k in range(NT):
            for m in range(LT):
                for f in (m * N + P * k, m * N + P * k + rows[k] - 1):
                    if f // BANK not in v_order:
                        v_order.append(f // BANK)

        def v_needed(k):
            return 1 + max(v_order.index(f // BANK) for m in range(LT)
                           for f in (m * N + P * k, m * N + P * k + rows[k] - 1))

        pool_tiles, act_tiles, dve_tiles = (list(r) for r in (
            range(0, NT - 2, 2), range(1, NT - 2, 2), range(NT - 2, NT)))

        def part_cols(j):
            q = j % AQ
            return q * BANK, (q + 1) * BANK

        def part_out(j):
            c0, c1 = part_cols(j)
            r = rows[j // AQ]
            return stage[j % len(stage)][0:r, 0:c1 - c0], ps[0:r, j % 2, 0:c1 - c0]

        NI = len(CH) * DT
        units = [(c * DT + d, k) for c in range(len(CH)) for d in range(DT) for k in range(NT)]
        per = DT * NT
        slot_units = [[] for _ in range(NG)]
        for c in range(len(CH) - 1):
            slots = list(range(CHG[c], CHG[c + 1]))
            for j in range(per):
                slot_units[slots[j * len(slots) // per]].append(units[c * per + j])
        tail_units = units[(len(CH) - 1) * per:]
        items_after = [[i for i, k in lot if k == NT - 1] for lot in slot_units]

        block = ctx.enter_context(nc.Block())

        @block.sync
        def _(sp):
            sp.dma_start(dst_i[0:ER, :], dst.rearrange("(p f) -> p f", p=ER)).then_inc(dst_in, 16)
            sp.wait_ge(prev_set, 1)
            with nc.allow_non_contiguous_dma("one column of the edge rows"):
                sp.dma_start(prev_i[1:ER, :], dst.rearrange("(p f) -> p f", p=ER)[0:ER - 1, EC - 1:EC]
                             ).then_inc(prev_in, 16)
            sp.dma_start(xs[:, 0:half, :], x[0:half * P, :].rearrange("(t p) d -> p t d", p=P)).then_inc(x_in, 16)
            sp.dma_start(src_i[0:ER, :], src.rearrange("(p f) -> p f", p=ER)).then_inc(src_in, 16)
            sp.wait_ge(lb1_zero, 1)
            for row in (0, 32):
                sp.dma_start(lb1r[row:row + 1, :], lb1.rearrange("(o d) -> o d", o=1)).then_inc(lb1_in, 16)
            sp.wait_ge(runs_asked, 1)
            sp.dma_start(xs[:, half:NT - 1, :], x[half * P:full, :].rearrange("(t p) d -> p t d", p=P)
                         ).then_inc(x_in2, 16)
            sp.dma_start(xs[0:rows[-1], NT - 1, :], x[full:N, :]).then_inc(x_in2, 16)
            sp.dma_start(w1s[:, :, :], w1.rearrange("(k p) n -> p k n", p=P)).then_inc(w1_in, 16)
            sp.dma_start(b2_all[:, :], lb2.rearrange("(o d) -> o d", o=1).broadcast_to([P, D])).then_inc(b2_in, 16)
            sp.wait_ge(h0_sum, NI)
            sp.dma_start(w2s[:, :, :], w2.rearrange("(k p) n -> p k n", p=P)).then_inc(w2_in, 16)
            for j in range(NJ):
                sp.wait_ge((A_act, A_dve)[j % 2], j // 2 + 1)
                kd = j // AQ
                c0, c1 = part_cols(j)
                sp.dma_start(a_spill[P * kd:P * kd + rows[kd], c0:c1], part_out(j)[0]
                             ).then_inc(spilled[j % len(stage)], 16)
            sp.wait_ge(z_sum, HT)
            sp.dma_start(lws[:, :, :], lw1.rearrange("(k p) n -> p k n", p=P)).then_inc(lw_in, 16)
            sp.dma_start(lw2s[:, :, :], lw2.rearrange("(k p) n -> p k n", p=P)).then_inc(lw_in, 16)
            for i in range(len(stage)):
                sp.wait_ge(spilled[i], 16 * (NJ // len(stage)))
            sp.wait_ge(w2h_set, HT)
            sp.wait_ge(w2l_set, HT)
            sp.dma_start(xs[:, 0:NT - 1, :], x[0:full, :].rearrange("(t p) d -> p t d", p=P)).then_inc(x_again, 16)
            sp.dma_start(xs[0:rows[-1], NT - 1, :], x[full:N, :]).then_inc(x_again, 16)
            sp.wait_ge(a1_first_used, 1)
            for i, k in enumerate(range(0, NT, 2)):
                if k == 8:
                    sp.wait_ge(z_part, len(CH))
                if rows[k + 1] == P:
                    sp.dma_start(A[0][:, k:k + 2, 0:AQ * BANK].bitcast(F32), a_spill[P * k:P * k + 2 * P, :].rearrange(
                        "(t p) n -> p t n", p=P)).then_inc(A_in[i], 16)
                else:
                    sp.dma_start(a_rows(k)[:, 0:AQ * BANK].bitcast(F32), a_spill[P * k:P * k + P, :]).then_inc(A_in[i], 16)
                    sp.dma_start(a_rows(k + 1)[0:rows[k + 1], 0:AQ * BANK].bitcast(F32), a_spill[P * k + P:N, :]).then_inc(A_in[i], 16)
            for k in range(NT):
                by, tiles = next(o for o in ((out_pool, pool_tiles), (out_act, act_tiles), (out_dve, dve_tiles)) if k in o[1])
                sp.wait_ge(by, tiles.index(k) + 1)
                sp.dma_start(out[P * k:P * k + rows[k], :], xs[0:rows[k], k, :]).then_inc(stored, 16)
            sp.wait_ge(stored, 16 * NT)
            sp.wait_ge(src_in, 16)

        @block.gpsimd
        def _(pl):
            n = [0]

            def link(ins):
                n[0] += 1
                ins.then_inc(pool, 1)
                pl.wait_ge(pool, n[0])

            nc.gpsimd.memset(prev_i[:, :], -1).then_inc(prev_set, 1)
            nc.gpsimd.iota(win_row[:, :], pattern=[[WIN, NW]], base=0, channel_multiplier=0,
                           allow_small_or_imprecise_dtypes=True).then_inc(const, 1)
            nc.gpsimd.iota(win_col[:, :], pattern=[[0, 1]], base=0, channel_multiplier=WIN,
                           allow_small_or_imprecise_dtypes=True).then_inc(const, 1)
            nc.gpsimd.memset(dst_f[:, EC:EC + 1], float(EC)).then_inc(const, 1)
            nc.gpsimd.memset(ones[:, :], 1.0).then_inc(const, 1)
            nc.gpsimd.iota(iota2[:, :, :], pattern=[[1, P], [0, 2]], base=0, channel_multiplier=0,
                           allow_small_or_imprecise_dtypes=True).then_inc(const, 1)
            link(nc.gpsimd.memset(ident[:, :], 0.0))
            nc.gpsimd.affine_select(out=ident[:, :], in_=ident[:, :], compare_op=ALU.not_equal, fill=1.0,
                                    base=0, pattern=[[-1, P]], channel_multiplier=1).then_inc(ident_set, 1)
            nc.gpsimd.memset(epsc[:, :], EPS).then_inc(const, 1)
            nc.gpsimd.memset(lb1r[:, :], 0.0).then_inc(lb1_zero, 1)
            link(nc.gpsimd.memset(one_r[:, :].bitcast(F32), 0.0))
            link(nc.gpsimd.memset(one_r[0:1, :].bitcast(F32), 1.0))
            link(nc.gpsimd.memset(one_r[32:33, :].bitcast(F32), 1.0))
            pl.wait_ge(start_set, 1)
            nc.gpsimd.indirect_dma_start(run_d[0:NW, :], None, dst.rearrange("(e o) -> e o", o=1),
                                         bass.IndirectOffsetOnAxis(ap=start_i[0:NW, :], axis=0)).then_inc(run_d_in, 16)
            nc.gpsimd.indirect_dma_start(run_s[0:NW, :], None, src.rearrange("(e o) -> e o", o=1),
                                         bass.IndirectOffsetOnAxis(ap=start_i[0:NW, :], axis=0)).then_inc(run_s_in, 16)
            nc.gpsimd.memset(asked[:, :], 0.0).then_inc(runs_asked, 1)
            for k in range(NT):
                pl.wait_ge(xh_set, k + 1)
                nc.gpsimd.tensor_tensor(xl[0:rows[k], k, :], xs[0:rows[k], k, :],
                                        xh[0:rows[k], k, :].bitcast(F32), ALU.subtract).then_inc(xl_set, 1)
            nc.gpsimd.iota(nodes[:, :], pattern=[[1, N]], base=0, channel_multiplier=0,
                           allow_small_or_imprecise_dtypes=True).then_inc(const, 1)
            nc.gpsimd.memset(gen_0[:, :], 0.0).then_inc(const, 1)
            for d in range(DT):
                pl.wait_ge(w1h_set, d + 1)
                nc.gpsimd.tensor_tensor(wl[:, :, d * P:d * P + P], w1s[:, d, :].rearrange("p (m c) -> p m c", c=P),
                                        wh[:, :, d * P:d * P + P].bitcast(F32), ALU.subtract).then_inc(w1l_set, 1)
            pl.wait_ge(h0_sum, NI)
            for k in range(NT):
                own = AT[0:rows[k], k, P * k:P * k + rows[k]]
                nc.gpsimd.tensor_tensor(own, own.bitcast(F32), ident[0:rows[k], 0:rows[k]], ALU.add
                                        ).then_inc(loops_set, 1)
            for t in range(HT):
                pl.wait_ge(w2h_set, t + 1)
                nc.gpsimd.tensor_tensor(wl[:, t, :], w2s[:, t, :], wh[:, t, :].bitcast(F32),
                                        ALU.subtract).then_inc(w2l_set, 1)
                if t < HT - 1:
                    pl.wait_ge(a1h_set, t + 1)
                    nc.gpsimd.tensor_tensor(a1(a1l, t), a32[t % 2][:, :], a1(a1h, t).bitcast(F32),
                                            ALU.subtract).then_inc(a1l_set, 1)
            pl.wait_ge(lwh_set, 3)
            nc.gpsimd.tensor_tensor(lw1l[:, :, :], lws[:, :, :], lw1h[:, :, :].bitcast(F32),
                                    ALU.subtract).then_inc(lwl_set, 1)
            nc.gpsimd.tensor_tensor(lw2l[:, :, :], lw2s[:, :, :], lw2h[:, :, :].bitcast(F32),
                                    ALU.subtract).then_inc(lwl_set, 1)
            low = slice(32, 33)
            pl.wait_ge(lwl_set, 2)
            nc.gpsimd.tensor_tensor(lb1p[low, :], lb1r[low, :], lb1p[low, :].bitcast(F32),
                                    ALU.subtract).then_inc(lwl_set, 1)
            pl.wait_ge(lwl_set, 3)

            def u_low(k):
                pl.wait_ge(uh_set, k + 1)
                nc.gpsimd.tensor_tensor(ul[0:rows[k], k, :], u32[0:rows[k], k % 2, :],
                                        uh[0:rows[k], k, :].bitcast(F32), ALU.subtract).then_inc(ul_set, 1)

            for k in range(NT):
                u_low(k)
            for k in pool_tiles:
                pl.wait_ge(ln2_aff, k + 1)
                r = rows[k]
                nc.gpsimd.tensor_scalar(xs[0:r, k, :], xs[0:r, k, :], ln_r[0:r, k, 0:1], ln_r[0:r, k, 1:2],
                                        ALU.mult, ALU.add).then_inc(out_pool, 1)

        @block.scalar
        def _(act):
            act.dma_start(eps_in[:, :], eps.rearrange("(o d) -> o d", o=1).broadcast_to([P, 1])).then_inc(eps_in_s, 16)
            for r, (v, t) in enumerate(((b1, HT), (g1, HT), (be1, HT), (b2, DT), (g2, DT), (be2, DT))):
                r0 = r * HT if r < 3 else 3 * HT + (r - 3) * DT
                act.dma_start(par_r[r0:r0 + t, :], v.rearrange("(t p) -> t p", p=P)).then_inc(par_in, 16)
            def x_high(k):
                if k == 0:
                    act.wait_ge(x_in, 16)
                if k == half:
                    act.wait_ge(x_in2, 32)
                nc.scalar.activation(xh[0:rows[k], k, :], xs[0:rows[k], k, :], ACT.Copy).then_inc(xh_set, 1)

            def group_out(g):
                act.wait_ge(built, g + 1)
                nc.scalar.activation(
                    AT[:, :, g * WG * WIN:(g + 1) * WG * WIN].rearrange("p k (w d) -> p k w d", w=WG),
                    ps[:, g % 2, 0:GCOLS].rearrange("p (w d k) -> p k w d", w=WG, k=NT), ACT.Copy
                ).then_inc(AT_set, 1)

            def w1_high(d):
                if d == 0:
                    act.wait_ge(w1_in, 16)
                nc.scalar.activation(wh[:, :, d * P:d * P + P], w1s[:, d, :].rearrange("p (m c) -> p m c", c=P),
                                     ACT.Copy).then_inc(w1h_set, 1)

            def h0_high(i):
                c, d = divmod(i, DT)
                c0, c1 = CH[c]
                act.wait_ge(h0_sum, i + 1)
                if i == 0:
                    act.wait_ge(const, 8)
                if i == NI - DT:
                    act.wait_ge(w1l_set, DT)
                nc.scalar.activation(h0h[c][:, d, :], ps[:, 2 + i % 6, 0:c1 - c0], ACT.Copy).then_inc(h0h_set, 1)

            for k in range(NT - 3):
                x_high(k)
            act.wait_ge(flag_set, 1)
            bad = act.value_load(flag[0:1, 0:1], min_val=0, max_val=1)
            with act.If(bad == 0):
                for g in range(NG):
                    group_out(g)
                    if g < 3:
                        x_high(NT - 3 + g)
                    if g >= 8 and g % 2 == 0 and (g - 8) // 2 < DT:
                        w1_high((g - 8) // 2)
                    for i in items_after[g]:
                        h0_high(i)
            with act.Else():
                for k in range(NT - 3, NT):
                    x_high(k)
                act.wait_ge(AT_set, NG)
                for d in range(DT):
                    w1_high(d)
                for i in range(NI - DT):
                    h0_high(i)
            for i in range(NI - DT, NI):
                h0_high(i)

            def affine(t):
                act.wait_ge(var_set, t + 1)
                nc.scalar.activation(std[:, :], mv[:, 1:2], ACT.Sqrt, bias=epsc[:, :]).then_inc(std_set, 1)
                act.wait_ge(aff_set, t + 1)
                o = a32[t % 2][:, :] if t < HT else h2[:, t - HT, :]
                if t < HT and t >= 2:
                    act.wait_ge(a1l_set, t - 1)
                if t == HT:
                    act.wait_ge(z_sum, HT)
                z0 = zbank(t, 0)
                n0 = CH[0][1]
                nc.scalar.activation(o[:, 0:n0], ps[:, z0, 0:n0], ACT.Relu, bias=col[:, 3:4],
                                     scale=col[:, 2:3]).then_inc(act_set, 1)
                nc.scalar.activation(o[:, n0:N].rearrange("p (b c) -> p b c", b=2),
                                     ps[:, z0 + 1:z0 + 3, 0:(N - n0) // 2], ACT.Relu, bias=col[:, 3:4],
                                     scale=col[:, 2:3]).then_inc(act_set, 1)

            def w2_high(t):
                act.wait_ge(z_sum, t + 1)
                if t == 0:
                    act.wait_ge(w2_in, 16)
                nc.scalar.activation(wh[:, t, :], w2s[:, t, :], ACT.Copy).then_inc(w2h_set, 1)

            def A_out(j):
                act.wait_ge(A_T, j + 1)
                if j >= len(stage):
                    act.wait_ge(spilled[j % len(stage)], 16 * (j // len(stage)))
                o, i = part_out(j)
                nc.scalar.activation(o, i, ACT.Copy).then_inc(A_act, 1)

            for j in range(0, JT, 2):
                A_out(j)
            for t in range(HT):
                affine(t)
                more = list(range((t + 1) * JT, min(NJ, (t + 2) * JT), 2))
                if more:
                    A_out(more[0])
                if t == 0:
                    act.wait_ge(h0_sum, NI)
                if t == HT // 2:
                    act.wait_ge(A_T, NJ)
                    act.wait_ge(deg_set, NT)
                act.wait_ge(act_set, 2 * t + 2)
                nc.scalar.activation(a1(a1h, t), a32[t % 2][:, :], ACT.Copy).then_inc(a1h_set, 1)
                w2_high(t)
                for j in more[1:]:
                    A_out(j)
            act.wait_ge(lw_in, 32)
            act.wait_ge(lb1_in, 32)
            act.wait_ge(a1l_set, HT - 1)
            act.wait_ge(a1l_last, 1)
            nc.scalar.activation(lw1h[:, :, :], lws[:, :, :], ACT.Copy).then_inc(lwh_set, 1)
            nc.scalar.activation(lw2h[:, :, :], lw2s[:, :, :], ACT.Copy).then_inc(lwh_set, 1)
            nc.scalar.activation(lb1p[:, :], lb1r[:, :], ACT.Copy).then_inc(lwh_set, 1)
            for t in range(HT, BT):
                affine(t)

            def late_out(i):
                act.wait_ge(late_T, i + 1)
                k = 2 * i
                o = ps[:, 2 + i, 0:2 * W_LATE].rearrange("p (t c) -> p t c", t=2)
                if rows[k + 1] == P:
                    nc.scalar.activation(A[0][:, k:k + 2, P * LATE:N], o, ACT.Copy).then_inc(late_set, 2)
                else:
                    for t in range(2):
                        r = rows[k + t]
                        nc.scalar.activation(a_rows(k + t)[0:r, P * LATE:N], o[0:r, t, :], ACT.Copy).then_inc(late_set, 1)

            def ln_root(k):
                act.wait_ge(ln_var, k + 1)
                r = rows[k]
                nc.scalar.activation(ln_std[0:r, k:k + 1], ln_mv[0:r, k, 1:2], ACT.Sqrt,
                                     bias=epsc[0:r, :]).then_inc(ln_std_s, 1)

            def ln_apply(k):
                act.wait_ge(ln_aff, k + 1)
                r = rows[k]
                nc.scalar.activation(xs[0:r, k, :], xs[0:r, k, :], ACT.Identity, bias=ln_r[0:r, k, 1:2],
                                     scale=ln_r[0:r, k, 0:1]).then_inc(x1_set, 1)

            def xt_high(k):
                r = rows[k]
                act.wait_ge(x1_T, k + 1)
                if k == 0:
                    act.wait_ge(lwl_set, 3)
                if k >= 2:
                    act.wait_ge(u_sum, k - 1)
                nc.scalar.activation(xth[:, k % 2, :].rearrange("p (d c) -> p d c", c=P)[:, :, 0:r],
                                     ps[:, 1, :].rearrange("p (d c) -> p d c", c=P)[:, :, 0:r],
                                     ACT.Copy).then_inc(xth_set, 1)

            def u_relu(k):
                r = rows[k]
                act.wait_ge(u_sum, k + 1)
                if k >= 2:
                    act.wait_ge(ul_set, k - 1)
                nc.scalar.activation(u32[0:r, k % 2, :], ps[0:r, 2, 0:L], ACT.Relu).then_inc(u32_set, 1)
                act.wait_ge(u32_set, k + 1)
                nc.scalar.activation(uh[0:r, k, :], u32[0:r, k % 2, :], ACT.Copy).then_inc(uh_set, 1)

            for i in range(3):
                late_out(i)
            for s in range(NT + 2):
                if s == 1:
                    for i in range(3, NT // 2):
                        late_out(i)
                if 0 <= s - 1 < NT:
                    xt_high(s - 1)
                if s < NT:
                    ln_root(s)
                    ln_apply(s)
                if 0 <= s - 2 < NT:
                    u_relu(s - 2)
            for i, b in enumerate(v_order):
                act.wait_ge(v_sum, i + 1)
                if i == 0:
                    act.wait_ge(u_sum, NT)
                f = slice(b * BANK, b * BANK + v_width[b])
                nc.scalar.activation(vh[:, f], ps[:, V0 + b, 0:v_width[b]], ACT.Copy).then_inc(vh_set, 1)

            sq = [u32[:, :, :].rearrange("p a b -> p (a b)"), lw1h[:, 0:2, :].rearrange("p a b -> p (a b)")]

            def ln2_root(k):
                act.wait_ge(ln2_mean, k + 1)
                if k == 0:
                    act.wait_ge(ul_set, NT)
                    act.wait_ge(u_sum, NT)
                r = rows[k]
                nc.scalar.activation(sq[k % 2][0:r, :], xs[0:r, k, :], ACT.Square, bias=ln_m[0:r, k, 1:2],
                                     accum_out=ln_q[0:r, k:k + 1]).then_inc(ln2_var, 1)
                act.wait_ge(ln2_var, k + 1)
                nc.scalar.activation(ln_std[0:r, k:k + 1], ln_q[0:r, k:k + 1], ACT.Sqrt,
                                     bias=epsc[0:r, :], scale=1.0 / D).then_inc(ln2_std, 1)

            def ln2_apply(k):
                act.wait_ge(ln2_aff, k + 1)
                r = rows[k]
                nc.scalar.activation(xs[0:r, k, :], xs[0:r, k, :], ACT.Identity, bias=ln_r[0:r, k, 1:2],
                                     scale=ln_r[0:r, k, 0:1]).then_inc(out_act, 1)

            for s in range(NT + 1):
                if s < NT:
                    ln2_root(s)
                if s >= 1 and s - 1 in act_tiles:
                    ln2_apply(s - 1)

        @block.vector
        def _(v):
            n = [0]

            def link(ins):
                n[0] += 1
                ins.then_inc(dve, 1)
                v.wait_ge(dve, n[0])

            v.wait_ge(dst_in, 16)
            v.wait_ge(const, 3)
            link(nc.vector.tensor_copy(dst_f[0:ER, 0:EC], dst_i[0:ER, :]))
            v.wait_ge(prev_in, 16)
            link(nc.vector.tensor_copy(prev_f[0:ER, :], prev_i[0:ER, :]))
            link(nc.vector.tensor_scalar(after[0:ER, :], win_row[0:ER, :], prev_f[0:ER, 0:1], None, ALU.is_gt))
            link(nc.vector.tensor_scalar(below[0:ER, :], win_row[0:ER, :], dst_f[0:ER, EC - 1:EC], None, ALU.is_gt))
            nc.vector.tensor_tensor(edge_row[0:ER, :], after[0:ER, :], below[0:ER, :],
                                    ALU.subtract).then_inc(rowsel, 1)
            v.wait_ge(rowed, 1)
            link(nc.vector.tensor_scalar(less[0:NW, :], ps[0:NW, 0, 0:EC], win_col[0:NW, 0:1], 0.0, ALU.is_lt,
                                         ALU.add, accum_out=lo_n[0:NW, 0:1]))
            link(nc.vector.tensor_tensor(lo_n[0:NW, 1:2], lo_n[0:NW, 0:1], ps[0:NW, 0, EC:EC + 1], ALU.add))
            link(nc.vector.tensor_scalar(lo_n[0:NW, 2:3], lo_n[0:NW, 1:2], float(E - RUN), 0.0, ALU.min, ALU.max))
            nc.vector.tensor_copy(start_i[0:NW, :], lo_n[0:NW, 2:3]).then_inc(start_set, 1)
            v.wait_ge(eps_in_s, 16)
            v.wait_ge(ident_set, 1)
            link(nc.vector.tensor_scalar(eps1[:, :], eps_in[:, :], 1.0, None, ALU.add))
            nc.vector.tensor_scalar(diag[:, :], ident[:, :], eps1[:, 0:1], None, ALU.mult).then_inc(diag_set, 1)
            v.wait_ge(run_d_in, 16)
            link(nc.vector.tensor_scalar(off[0:NW, :], run_d[0:NW, :], win_col[0:NW, 0:1], float(NT), ALU.subtract,
                                         ALU.mult))
            v.wait_ge(run_s_in, 16)
            nc.vector.tensor_scalar(hi_i[0:NW, :], run_s[0:NW, :], 7, None, ALU.logical_shift_right).then_inc(dve, 1)
            nc.vector.tensor_scalar(lo_i[0:NW, :], run_s[0:NW, :], P - 1, None, ALU.bitwise_and).then_inc(dve, 1)
            n[0] += 2
            v.wait_ge(dve, n[0] - 1)
            link(nc.vector.scalar_tensor_tensor(out=key[0:NW, :], in0=hi_i[0:NW, :], scalar=1.0, in1=off[0:NW, :],
                                                op0=ALU.mult, op1=ALU.add))
            nc.vector.tensor_copy(lo_f[0:NW, :], lo_i[0:NW, :]).then_inc(keys_set, 1)
            nc.vector.tensor_scalar(over[0:NW, :], key[0:NW, :], float(KEYS), None, ALU.is_ge).then_inc(dve, 1)
            n[0] += 1
            link(nc.vector.tensor_scalar(under[0:NW, :], key[0:NW, :], 0.0, None, ALU.is_lt))
            nc.vector.tensor_tensor_reduce(out=outside[0:NW, :], in0=over[0:NW, :], in1=under[0:NW, :], scale=1.0,
                                           scalar=0.0, op0=ALU.add, op1=ALU.add,
                                           accum_out=n_out[0:NW, :]).then_inc(n_out_set, 1)
            v.wait_ge(par_T, 1)
            nc.vector.tensor_copy(par[:, :], ps[:, 1, 0:3 * BT]).then_inc(par_set, 1)
            v.wait_ge(keys_T, 1)
            q = ps[:, 0, 0:4 * NW].rearrange("p (a c w) -> p a w c", a=2, c=2)
            link(nc.vector.tensor_copy(keyT[:, :, :], q[:, 0]))
            link(nc.vector.tensor_copy(loT[:, :, :], q[:, 1]))
            v.wait_ge(counted, 1)
            nc.vector.tensor_scalar(flag[0:1, :], ps[0:1, 1, 0:1], float(NW * RUN - E), None,
                                    ALU.not_equal).then_inc(flag_set, 1)

            def one_hots(g):
                if g >= 2:
                    v.wait_ge(built, g - 1)
                w = slice(g * WG, (g + 1) * WG)
                nc.vector.tensor_tensor(
                    hot_s[g % 2][:, :, :, :], iota2[:, None, :, :].broadcast_to([P, WG, P, 2]),
                    loT[:, w, None, :].broadcast_to([P, WG, P, 2]), ALU.is_equal).then_inc(hot, 1)
                nc.vector.tensor_tensor(
                    hot_k[g % 2][:, :, :, :], iota2[:, None, 0:KEYS, :].broadcast_to([P, WG, KEYS, 2]),
                    keyT[:, w, None, :].broadcast_to([P, WG, KEYS, 2]), ALU.is_equal).then_inc(hot, 1)

            def h0_low(i):
                c, d = divmod(i, DT)
                c0, c1 = CH[c]
                v.wait_ge(h0h_set, i + 1)
                nc.vector.tensor_tensor(h0l[c][:, d, :], ps[:, 2 + i % 6, 0:c1 - c0],
                                        h0h[c][:, d, :].bitcast(F32), ALU.subtract).then_inc(h0l_set, 1)

            EARLY = 2
            for g in range(EARLY):
                one_hots(g)
            v.wait_ge(flag_set, 1)
            bad = v.value_load(flag[0:1, 0:1], min_val=0, max_val=1)
            with v.If(bad == 0):
                late = []
                for g in range(NG):
                    if g >= EARLY:
                        one_hots(g)
                    while late and late[0][0] <= g:
                        h0_low(late.pop(0)[1])
                    late += [(g + 2, i) for i in items_after[g]]
                for _, i in late:
                    h0_low(i)
            with v.Else():
                v.wait_ge(src_in, 16)
                v.wait_ge(const, 8)
                nc.vector.tensor_copy(gen_src[0:ER, :], src_i[0:ER, :]).then_inc(gen_copied, 1)
                with v.Fori(0, NT) as h:
                    with v.Fori(0, EC) as f:
                        v.wait_ge(gen_copied, h * 4 + 1)
                        v.wait_ge(gen_used, h * (EC + 1) + f + 1)
                        nc.vector.tensor_scalar(gen_s[0:ER, :], iota2[0:ER, :, 0], gen_src[0:ER, bass.ds(f, 1)],
                                                None, ALU.is_equal).then_inc(gen_hot, 1)
                        nc.vector.tensor_scalar(gen_d[0:ER, :], nodes[0:ER, :], dst_f[0:ER, bass.ds(f, 1)],
                                                None, ALU.is_equal).then_inc(gen_hot, 1)
                    v.wait_ge(gen_sum, h + 1)
                    for c, (c0, c1) in enumerate(CH):
                        nc.vector.tensor_copy(AT[:, bass.ds(h, 1), c0:c1],
                                              ps[:, 2 + c, None, 0:c1 - c0]).then_inc(gen_copied, 1)
                    nc.vector.tensor_scalar(gen_src[0:ER, :], gen_src[0:ER, :], -float(P), None,
                                            ALU.add).then_inc(gen_copied, 1)
                v.wait_ge(gen_copied, 4 * NT + 1)
                nc.vector.memset(n_out[:, :], 0.0).then_inc(AT_set, NG)
                for i in range(NI - DT):
                    h0_low(i)
            for i in range(NI - DT, NI):
                h0_low(i)

            def batch_norm(t):
                if t < BT - 1:
                    v.wait_ge(z_sum, t + 1)
                if t == 0:
                    v.wait_ge(par_set, 1)
                i = t if t < HT else t + 2 * HT
                step = HT if t < HT else DT
                b, g, be = (par[:, i + j * step:i + j * step + 1] for j in range(3))
                for n_c, c in enumerate(last_order if t == BT - 1 else range(len(CH))):
                    c0, c1 = CH[c]
                    if t == BT - 1:
                        v.wait_ge(z_part, n_c + 1)
                    link(nc.vector.bn_stats(stats[:, 6 * c:6 * c + 6], ps[:, zbank(t, c), 0:c1 - c0]))
                nc.vector.bn_aggr(mv[:, :], stats[:, :]).then_inc(var_set, 1)
                v.wait_ge(var_set, t + 1)
                link(nc.vector.tensor_tensor(col[:, 0:1], mv[:, 0:1], b, ALU.add))
                link(nc.vector.tensor_tensor(col[:, 1:2], b, col[:, 0:1], ALU.subtract))
                v.wait_ge(std_set, t + 1)
                link(nc.vector.reciprocal(rstd[:, :], std[:, :]))
                if t >= 1:
                    v.wait_ge(act_set, 2 * t)
                link(nc.vector.tensor_tensor(col[:, 2:3], rstd[:, :], g, ALU.mult))
                nc.vector.scalar_tensor_tensor(out=col[:, 3:4], in0=col[:, 1:2], scalar=col[:, 2:3], in1=be,
                                               op0=ALU.mult, op1=ALU.add).then_inc(aff_set, 1)

            def A_out(j):
                v.wait_ge(A_T, j + 1)
                if j >= len(stage):
                    v.wait_ge(spilled[j % len(stage)], 16 * (j // len(stage)))
                o, i = part_out(j)
                nc.vector.tensor_copy(o, i).then_inc(A_dve, 1)

            v.wait_ge(loops_set, NT)
            def degree(k):
                nc.vector.tensor_reduce(deg1[:, k:k + 1], AT[:, k, :].bitcast(F32), AX_X, ALU.add).then_inc(deg_set, 1)

            for t in range(-1, HT):
                if t >= 0:
                    batch_norm(t)
                for j in range((t + 1) * JT + 1, min(NJ, (t + 2) * JT), 2):
                    A_out(j)
                    if j % JT == 1:
                        degree(2 * t + 2)
                        degree(2 * t + 3)
            v.wait_ge(a1h_set, HT)
            nc.vector.tensor_tensor(a1(a1l, HT - 1), a32[(HT - 1) % 2][:, :], a1(a1h, HT - 1).bitcast(F32),
                                    ALU.subtract).then_inc(a1l_last, 1)
            for t in range(HT, BT):
                batch_norm(t)

            def ln_stats(k):
                r = rows[k]
                v.wait_ge(h2_T, k + 1)
                nc.vector.scalar_tensor_tensor(out=xs[0:r, k, :], in0=xs[0:r, k, :], scalar=2.0,
                                               in1=ps[0:r, 0, :], op0=ALU.mult, op1=ALU.add).then_inc(h2_used, 1)
                v.wait_ge(h2_used, k + 1)
                link(nc.vector.bn_stats(ln_s[0:r, k, :], xs[0:r, k, :]))
                nc.vector.bn_aggr(ln_mv[0:r, k, :], ln_s[0:r, k, :]).then_inc(ln_var, 1)

            def ln_scale(k, root, done):
                r = rows[k]
                v.wait_ge(root, k + 1)
                link(nc.vector.reciprocal(ln_r[0:r, k, 0:1], ln_std[0:r, k:k + 1]))
                nc.vector.scalar_tensor_tensor(out=ln_r[0:r, k, 1:2], in0=ln_mv[0:r, k, 0:1], scalar=-1.0,
                                               in1=ln_r[0:r, k, 0:1], op0=ALU.mult, op1=ALU.mult).then_inc(done, 1)

            def xt_low(k):
                r = rows[k]
                v.wait_ge(xth_set, k + 1)
                nc.vector.tensor_tensor(xtl[:, k % 2, :].rearrange("p (d c) -> p d c", c=P)[:, :, 0:r],
                                        ps[:, 1, :].rearrange("p (d c) -> p d c", c=P)[:, :, 0:r],
                                        xth[:, k % 2, :].rearrange("p (d c) -> p d c", c=P)[:, :, 0:r].bitcast(F32),
                                        ALU.subtract).then_inc(xtl_set, 1)

            v.wait_ge(x_again, 32)
            for s in range(NT + 1):
                if s < NT:
                    ln_stats(s)
                    ln_scale(s, ln_std_s, ln_aff)
                if s >= 1:
                    xt_low(s - 1)

            def base(k):
                r = rows[k]
                v.wait_ge(x1_T, k + 1)
                nc.vector.scalar_tensor_tensor(out=xs[0:r, k, :], in0=b2_all[0:r, :], scalar=deg1[0:r, k:k + 1],
                                               in1=xs[0:r, k, :], op0=ALU.mult, op1=ALU.add).then_inc(base_set, 1)

            v.wait_ge(b2_in, 16)
            v.wait_ge(deg_set, NT)
            for k in range(NT):
                base(k)
            for i, b in enumerate(v_order):
                v.wait_ge(vh_set, i + 1)
                f = slice(b * BANK, b * BANK + v_width[b])
                nc.vector.tensor_tensor(vl[:, f], ps[:, V0 + b, 0:v_width[b]], vh[:, f].bitcast(F32),
                                        ALU.subtract).then_inc(vl_set, 1)

            def ln2_sum(k):
                r = rows[k]
                v.wait_ge(y_sum, k + 1)
                link(nc.vector.tensor_tensor_reduce(out=xs[0:r, k, :], in0=ps[0:r, k % V0, :], in1=xs[0:r, k, :],
                                                    scale=1.0, scalar=0.0, op0=ALU.add, op1=ALU.add,
                                                    accum_out=ln_m[0:r, k, 0:1]))
                nc.vector.tensor_scalar(ln_m[0:r, k, 1:2], ln_m[0:r, k, 0:1], -1.0 / D, None,
                                        ALU.mult).then_inc(ln2_mean, 1)

            def ln2_scale(k):
                r = rows[k]
                v.wait_ge(ln2_std, k + 1)
                link(nc.vector.reciprocal(ln_r[0:r, k, 0:1], ln_std[0:r, k:k + 1]))
                nc.vector.tensor_tensor(ln_r[0:r, k, 1:2], ln_m[0:r, k, 1:2], ln_r[0:r, k, 0:1],
                                        ALU.mult).then_inc(ln2_aff, 1)

            v.wait_ge(base_set, NT)
            def ln2_apply(k):
                r = rows[k]
                v.wait_ge(ln2_aff, k + 1)
                nc.vector.tensor_scalar(xs[0:r, k, :], xs[0:r, k, :], ln_r[0:r, k, 0:1], ln_r[0:r, k, 1:2],
                                        ALU.mult, ALU.add).then_inc(out_dve, 1)

            for s in range(NT + 1):
                if s < NT:
                    ln2_sum(s)
                if s >= 1:
                    ln2_scale(s - 1)
                    if s - 1 in dve_tiles:
                        ln2_apply(s - 1)

        @block.tensor
        def _(pe):
            mm = nc.tensor.matmul
            pe.wait_ge(rowsel, 1)
            mm(ps[0:NW, 0, 0:EC], edge_row[0:ER, :], dst_f[0:ER, 0:EC], start=True, stop=True)
            mm(ps[0:NW, 0, EC:EC + 1], below[0:ER, :], dst_f[0:ER, EC:EC + 1], start=True, stop=True).then_inc(rowed, 1)

            def own(i, k0=0, k1=NT):
                c, d = divmod(i, DT)
                c0, c1 = CH[c]
                if i >= RING:
                    pe.wait_ge(h0l_set, i - RING + 1)
                for k in range(max(k0, c0 // P), min(k1, cdiv(c1, P))):
                    a, b = max(c0, P * k), min(c1, P * k + P)
                    mm(ps[:, 2 + i % RING, a - c0:b - c0], xs[0:rows[k], k, d * P:d * P + P],
                       diag[0:rows[k], a - P * k:b - P * k], start=(a == c0), stop=False, skip_group_check=True)

            pe.wait_ge(diag_set, 1)
            pe.wait_ge(x_in, 16)
            for i in range(DT):
                own(i, 0, half)
            pe.wait_ge(ident_set, 1)
            pe.wait_ge(par_in, 6 * 16)
            nc.tensor.transpose(ps[:, 1, 0:3 * BT], par_r[0:3 * BT, :], ident[0:3 * BT, 0:3 * BT]).then_inc(par_T, 1)
            pe.wait_ge(keys_set, 1)
            for a, s in enumerate((key, lo_f)):
                for c in range(2):
                    o = (2 * a + c) * NW
                    last = nc.tensor.transpose(ps[:, 0, o:o + NW], s[0:NW, c * P:c * P + P], ident[0:NW, 0:NW])
            last.then_inc(keys_T, 1)
            pe.wait_ge(const, 5)
            pe.wait_ge(n_out_set, 1)
            pe.wait_ge(par_set, 1)
            mm(ps[0:1, 1, 0:1], n_out[0:NW, :], ones[0:NW, :], start=True, stop=True).then_inc(counted, 1)
            own(DT, 0, half)

            def build(g):
                pe.wait_ge(hot, 2 * g + 2)
                if g >= 2:
                    pe.wait_ge(AT_set, g - 1)
                for w in range(WG):
                    for c in range(2):
                        last = mm(ps[:, g % 2, w * KEYS:(w + 1) * KEYS], hot_s[g % 2][:, w, :, c],
                                  hot_k[g % 2][:, w, :, c], start=(c == 0), stop=(c == 1))
                last.then_inc(built, 1)

            def aggregate(i, k):
                c, d = divmod(i, DT)
                c0, c1 = CH[c]
                o = ps[:, 2 + i % RING, 0:c1 - c0]
                if k == 0:
                    if i >= RING:
                        own(i)
                    pe.wait_ge(AT_set, CHG[c])
                    if i < RING:
                        own(i, half)
                if i == 0:
                    pe.wait_ge(xl_set, k + 1)
                r = rows[k]
                for j, part in enumerate((xh, xl)):
                    last = mm(o, part[0:r, k, d * P:d * P + P], AT[0:r, k, c0:c1], start=False,
                              stop=(k == NT - 1 and j == 1), skip_group_check=True)
                if k == NT - 1:
                    last.then_inc(h0_sum, 1)

            for g in range(2):
                build(g)
            pe.wait_ge(flag_set, 1)
            bad = pe.value_load(flag[0:1, 0:1], min_val=0, max_val=1)
            with pe.If(bad == 0):
                for g in range(NG):
                    if g >= 2:
                        build(g)
                    if g >= 2 and DT + g - 1 < RING:
                        own(DT + g - 1, 0, half)
                    for u in slot_units[g]:
                        aggregate(*u)
            with pe.Else():
                with pe.Fori(0, NT) as h:
                    pe.wait_ge(gen_copied, h * 4 + 1)
                    for c, (c0, c1) in enumerate(CH):
                        last = mm(ps[:, 2 + c, 0:c1 - c0], gen_0[0:ER, 0:P], gen_0[0:ER, 0:c1 - c0], start=True,
                                  stop=False, skip_group_check=True)
                    last.then_inc(gen_used, 1)
                    with pe.Fori(0, EC) as f:
                        pe.wait_ge(gen_hot, (h * EC + f) * 2 + 2)
                        for c, (c0, c1) in enumerate(CH):
                            last = mm(ps[:, 2 + c, 0:c1 - c0], gen_s[0:ER, :], gen_d[0:ER, c0:c1], start=False,
                                      stop=False, skip_group_check=True)
                        last.then_inc(gen_used, 1)
                    for c, (c0, c1) in enumerate(CH):
                        last = mm(ps[:, 2 + c, 0:c1 - c0], gen_0[0:ER, 0:P], gen_0[0:ER, 0:c1 - c0], start=False,
                                  stop=True, skip_group_check=True)
                    last.then_inc(gen_sum, 1)
                pe.wait_ge(AT_set, NG)
                for i in range(RING):
                    own(i, 0, half)
                for u in units[0:(len(CH) - 1) * per]:
                    aggregate(*u)
            for u in tail_units:
                aggregate(*u)

            def A_rows(j):
                kd, q = divmod(j, AQ)
                pe.wait_ge(loops_set, kd + 1)
                if j >= 2:
                    pe.wait_ge((A_act, A_dve)[j % 2], j // 2)
                for ks in range(4 * q, 4 * q + 4):
                    o = (ks - 4 * q) * P
                    last = nc.tensor.transpose(ps[0:rows[kd], j % 2, o:o + rows[ks]],
                                               AT[0:rows[ks], ks, P * kd:P * kd + rows[kd]].bitcast(F32),
                                               ident[0:rows[ks], 0:rows[ks]])
                last.then_inc(A_T, 1)

            pe.wait_ge(w1l_set, DT)
            pair_at = [(1, DT - 1), (2, DT - 1)]
            for t in range(HT):
                if t >= 2:
                    pe.wait_ge(act_set, 2 * t - 2)
                for c, (c0, c1) in enumerate(CH):
                    if t == 0:
                        pe.wait_ge(h0l_set, max(DT * (c + 1), 7 + c))
                    for d in range(DT):
                        for j, (w, h) in enumerate(((wh, h0h), (wl, h0h), (wh, h0l))):
                            last = mm(ps[:, zbank(t, c), 0:c1 - c0], w[:, t, d * P:d * P + P], h[c][:, d, :],
                                      start=(d == 0 and j == 0), stop=(d == DT - 1 and j == 2))
                        if c == len(CH) - 1 and d == DT - 1:
                            last.then_inc(z_sum, 1)
                        if (c, d) in pair_at:
                            j0 = t * JT + 2 * pair_at.index((c, d))
                            for j in range(j0, min(NJ, j0 + 2)):
                                A_rows(j)

            mid = HT // 2
            runs = [(t, 0, HT) for t in range(HT, BT - 2)]
            runs += [(t, k0, k0 + mid) for k0 in (0, mid) for t in (BT - 2, BT - 1)]

            def hidden2(t, k, j, c):
                w, a = ((wh, a1h), (wl, a1h), (wh, a1l))[j]
                c0, c1 = CH[c]
                return mm(ps[:, zbank(t, c), 0:c1 - c0], w[:, k, (t - HT) * P:(t - HT + 1) * P], a1(a, k)[:, c0:c1],
                          start=(k == 0 and j == 0), stop=(k == HT - 1 and j == 2))

            for t, k0, k1 in runs:
                if k0 == 0:
                    pe.wait_ge(act_set, 2 * t - 2)
                for k in range(k0, k1):
                    if t == HT:
                        pe.wait_ge(w2l_set, k + 1)
                        if k < HT - 1:
                            pe.wait_ge(a1l_set, k + 1)
                        else:
                            pe.wait_ge(a1l_last, 1)
                    if (t, k1) != (BT - 1, HT):
                        for j in range(3):
                            for c in range(len(CH)):
                                last = hidden2(t, k, j, c)
                if (t, k1) == (BT - 1, HT):
                    for c in last_order:
                        for k in range(k0, k1):
                            for j in range(3):
                                last = hidden2(t, k, j, c)
                        last.then_inc(z_part, 1)
                elif k1 == HT:
                    last.then_inc(z_sum, 1)
                elif t == BT - 1:
                    last.then_inc(a1_first_used, 1)

            def late_rows(i):
                for t in range(2):
                    kd = 2 * i + t
                    for ks in range(LATE, NT):
                        o = t * W_LATE + (ks - LATE) * P
                        last = nc.tensor.transpose(ps[0:rows[kd], 2 + i, o:o + rows[ks]],
                                                   AT[0:rows[ks], ks, P * kd:P * kd + rows[kd]].bitcast(F32),
                                                   ident[0:rows[ks], 0:rows[ks]])
                last.then_inc(late_T, 1)

            def h2_rows(k):
                r = rows[k]
                if k < 2:
                    assert CH[0][1] >= P
                    pe.wait_ge(act_set, 2 * BT - 1 + k)
                if k >= 1:
                    pe.wait_ge(h2_used, k)
                for m in range(DT):
                    last = nc.tensor.transpose(ps[0:r, 0, m * P:m * P + P], h2[:, m, P * k:P * k + r], ident[:, :])
                last.then_inc(h2_T, 1)

            def x1_cols(k):
                r = rows[k]
                pe.wait_ge(x1_set, k + 1)
                if k >= 1:
                    pe.wait_ge(xtl_set, k)
                for d in range(DT):
                    last = nc.tensor.transpose(ps[:, 1, d * P:d * P + r], xs[0:r, k, d * P:d * P + P],
                                               ident[0:r, 0:r])
                last.then_inc(x1_T, 1)

            def hidden(k):
                r = rows[k]
                pe.wait_ge(xtl_set, k + 1)
                if k == 0:
                    pe.wait_ge(lwl_set, 3)
                if k == 0:
                    pe.wait_ge(late_set, 2)
                if k >= 1:
                    pe.wait_ge(u32_set, k)
                o = ps[0:r, 2, 0:L]
                mm(o, one_r[:, 0:r], lb1p[:, :], start=True, stop=False)
                for d in range(DT):
                    for j, (xt, w) in enumerate(((xth, lw1h), (xtl, lw1h), (xth, lw1l))):
                        last = mm(o, xt[:, k % 2, d * P:d * P + r], w[:, d, :], start=False,
                                  stop=(d == DT - 1 and j == 2))
                last.then_inc(u_sum, 1)

            def own_and_neighbours(k):
                r = rows[k]
                pe.wait_ge(ul_set, k + 1)
                if k == 0:
                    pe.wait_ge(late_set, NT)
                pe.wait_ge(A_in[k // 2], 16 if rows[k - k % 2 + 1] == P else 32)

                def product(m, j, b, c0, c1):
                    f = m * N - b * BANK
                    return mm(ps[:, V0 + b, f + c0:f + c1], (uh, ul)[j][0:r, k, m * P:m * P + P], a_rows(k)[0:r, c0:c1],
                              start=(k == 0 and j == 0 and v_first[b] == m), stop=(k == NT - 1 and j == 1),
                              skip_group_check=True)

                if k < NT - 1:
                    for m in range(LT):
                        for j in range(2):
                            for mb, b, c0, c1 in v_blocks:
                                if mb == m:
                                    product(m, j, b, c0, c1)
                    return
                for bank in v_order:
                    for m, b, c0, c1 in v_blocks:
                        if b == bank:
                            for j in range(2):
                                last = product(m, j, b, c0, c1)
                    last.then_inc(v_sum, 1)

            pe.wait_ge(act_set, 2 * BT - 2)
            for i in range(3):
                late_rows(i)
            def keep_warm(n):
                for _ in range(n):
                    mm(ps[:, 1, :], wh[:, 0, 0:P], wh[:, 0, :], start=True, stop=True)

            keep_warm(6)
            for s in range(-1, NT + 3):
                if s == 0:
                    pe.wait_ge(act_set, 2 * BT)
                    for i in range(3, NT // 2):
                        late_rows(i)
                if s == 1:
                    keep_warm(6)
                if 0 <= s - 1 < NT:
                    x1_cols(s - 1)
                if 0 <= s - 2 < NT:
                    hidden(s - 2)
                if s + 1 < NT:
                    h2_rows(s + 1)
                if s >= 3:
                    own_and_neighbours(s - 3)

            for k in range(NT):
                r = rows[k]
                pe.wait_ge(vl_set, v_needed(k))
                if k >= V0:
                    pe.wait_ge(ln2_mean, k - V0 + 1)
                for m in range(LT):
                    f = m * N + P * k
                    for j, (part, w) in enumerate(((vh, lw2h), (vl, lw2h), (vh, lw2l))):
                        last = mm(ps[0:r, k % V0, :], part[:, f:f + r], w[:, m, :],
                                  start=(m == 0 and j == 0), stop=(m == LT - 1 and j == 2))
                last.then_inc(y_sum, 1)


_INS = ["x", "src", "dst", "L0_gnn_eps", "L0_gnn_W1", "L0_gnn_b1", "L0_gnn_g1", "L0_gnn_be1", "L0_gnn_W2",
        "L0_gnn_b2", "L0_gnn_g2", "L0_gnn_be2", "L1_gnn_W1", "L1_gnn_b1", "L1_gnn_W2", "L1_gnn_b2"]


def kernel(**inputs):
    import numpy as np
    import concourse.bacc as bacc
    from concourse.bass_utils import run_bass_kernel_spmd

    nc = bacc.Bacc("TRN2", target_bir_lowering=False, num_devices=1)
    arrays, args = {}, []
    for name in _INS:
        a = np.ascontiguousarray(inputs[name]).reshape(np.shape(inputs[name]) or (1,))
        arrays[f"in_{name}"] = a
        args.append(nc.dram_tensor(f"in_{name}", a.shape, mybir.dt.from_np(a.dtype), kind="ExternalInput").ap())
    n, d = inputs["x"].shape
    args.append(nc.dram_tensor("out_0", (n, d), F32, kind="ExternalOutput").ap())
    args.append(nc.dram_tensor("a_spill", (n, n // BANK * BANK), F32, kind="Internal").ap())
    gnn_kernel(nc, *args)
    r = run_bass_kernel_spmd(nc, [arrays], core_ids=[0])
    return r.results[0]["out_0"]
```
